# Optimizing a Trainium2 kernel written in Bass

```python
import numpy as np
import jax
import jax.numpy as jnp

def _softmax(x, axis=-1):
    return jax.nn.softmax(x, axis=axis)
def _gelu(x):
    return jax.nn.gelu(x, approximate=True)
def _silu(x):
    return jax.nn.silu(x)
def _sigmoid(x):
    return jax.nn.sigmoid(x)
def _layernorm(x, axis=-1, eps=1e-5):
    m = jnp.mean(x, axis=axis, keepdims=True)
    v = jnp.var(x, axis=axis, keepdims=True)
    return (x - m) / jnp.sqrt(v + eps)
def _scatter_add(tgt, idx, src, axis=0):
    return tgt.at[idx].add(src)
def _segment_sum(src, seg, n):
    return jax.ops.segment_sum(src, seg, n)

kernel_name = 'mk_conv_preact_d2_conv_nchw32_1de7f5'

def setup_inputs(seed: int = 0):
    np.random.seed(seed)
    _w = jnp.asarray
    def _rec_inputs():
        import jax
        import jax.numpy as jnp
        _gk = jax.random.key(seed)
        x = -0.000125 + 0.9999 * jax.random.normal(jax.random.fold_in(_gk, 1), (16, 32, 256, 256), jnp.float32)
        return x
    x = _rec_inputs()
    def _L0_conv_setup():
        import jax, jax.numpy as jnp
        import numpy as np
        from jax import lax
        B, C, H, W = (16, 32, 256, 256)
        N_OPS = 4
        HIDDEN = 64
        TOPK = 2
        TEMP = 1.0
        DIL = 2
        EPS = 1e-06

        def _conv2d(x, w, b, dil=1):
            out = lax.conv_general_dilated(x, w, window_strides=(1, 1), padding='SAME', rhs_dilation=(dil, dil), dimension_numbers=('NCHW', 'OIHW', 'NCHW'))
            return out + b[None, :, None, None]

        def _avgpool3x3(x):
            s = lax.reduce_window(x, 0.0, lax.add, (1, 1, 3, 3), (1, 1, 1, 1), 'SAME')
            return s / 9.0

        def _forward(x, gw1, gb1, gw2, gb2, sw, sb, k1, kb1, k2, kb2):
            g = jnp.mean(x, axis=(2, 3))
            h = jax.nn.relu(g @ gw1.T + gb1)
            glog = h @ gw2.T + gb2
            slog = jnp.einsum('bchw,nc->bnhw', x, sw) + sb[None, :, None, None]
            logits = (glog[:, :, None, None] + slog) / TEMP
            weights = jax.nn.softmax(logits, axis=1)
            wt = jnp.moveaxis(weights, 1, -1)
            _, idx = lax.top_k(wt, TOPK)
            mask = jnp.sum(jax.nn.one_hot(idx, N_OPS, dtype=wt.dtype), axis=-2)
            w = wt * mask
            denom = jnp.maximum(jnp.sum(w, axis=-1, keepdims=True), EPS)
            w = jnp.moveaxis(w / denom, -1, 1)
            out = x * w[:, 0:1]
            out = out + _conv2d(x, k1, kb1, 1) * w[:, 1:2]
            out = out + _conv2d(x, k2, kb2, DIL) * w[:, 2:3]
            out = out + _avgpool3x3(x) * w[:, 3:4]
            return out
        key = jax.random.key(seed)
        ks = jax.random.split(key, 12)
        sc = 0.05
        return {'x': jax.random.normal(ks[0], (B, C, H, W), jnp.float32), 'gw1': jax.random.normal(ks[1], (HIDDEN, C), jnp.float32) * sc, 'gb1': jnp.zeros((HIDDEN,), jnp.float32), 'gw2': jax.random.normal(ks[2], (N_OPS, HIDDEN), jnp.float32) * sc, 'gb2': jnp.zeros((N_OPS,), jnp.float32), 'sw': jax.random.normal(ks[3], (N_OPS, C), jnp.float32) * sc, 'sb': jnp.zeros((N_OPS,), jnp.float32), 'k1': jax.random.normal(ks[4], (C, C, 3, 3), jnp.float32) * sc, 'kb1': jnp.zeros((C,), jnp.float32), 'k2': jax.random.normal(ks[5], (C, C, 3, 3), jnp.float32) * sc, 'kb2': jnp.zeros((C,), jnp.float32)}
    _L0_conv_all = _L0_conv_setup()
    _L0_conv_in = {k: v for k, v in _L0_conv_all.items() if k in ('gw1', 'gb1', 'gw2', 'gb2', 'sw', 'sb', 'k1', 'kb1', 'k2', 'kb2', )}
    del _L0_conv_all

    def _L1_conv_setup():
        import jax, jax.numpy as jnp
        import numpy as np
        KERNEL = (3, 3)
        STRIDE = (1, 1)
        PADDING = ((1, 1), (1, 1))
        DILATION = (1, 1)
        key = jax.random.key(seed)
        k1, k2, k3 = jax.random.split(key, 3)
        x = jax.random.normal(k1, (16, 32, 224, 224), dtype=jnp.float32)
        weight = jax.random.normal(k2, (32, 32, 3, 3), dtype=jnp.float32) * 0.05
        bias = jax.random.normal(k3, (32,), dtype=jnp.float32) * 0.05
        return {'x': x, 'weight': weight, 'bias': bias}
    _L1_conv_all = _L1_conv_setup()
    _L1_conv_in = {k: v for k, v in _L1_conv_all.items() if k in ('weight', 'bias', )}
    del _L1_conv_all

    return {
        "x": x,
        "L0_conv_gw1": _L0_conv_in["gw1"],
        "L0_conv_gb1": _L0_conv_in["gb1"],
        "L0_conv_gw2": _L0_conv_in["gw2"],
        "L0_conv_gb2": _L0_conv_in["gb2"],
        "L0_conv_sw": _L0_conv_in["sw"],
        "L0_conv_sb": _L0_conv_in["sb"],
        "L0_conv_k1": _L0_conv_in["k1"],
        "L0_conv_kb1": _L0_conv_in["kb1"],
        "L0_conv_k2": _L0_conv_in["k2"],
        "L0_conv_kb2": _L0_conv_in["kb2"],
        "L1_conv_weight": _L1_conv_in["weight"],
        "L1_conv_bias": _L1_conv_in["bias"],
    }

def reference(x, L0_conv_gw1, L0_conv_gb1, L0_conv_gw2, L0_conv_gb2, L0_conv_sw, L0_conv_sb, L0_conv_k1, L0_conv_kb1, L0_conv_k2, L0_conv_kb2, L1_conv_weight, L1_conv_bias):
    import jax
    import jax.numpy as jnp
    def _L0_conv_ref(x, gw1, gb1, gw2, gb2, sw, sb, k1, kb1, k2, kb2):
        import jax, jax.numpy as jnp
        import numpy as np
        from jax import lax
        B, C, H, W = (16, 32, 256, 256)
        N_OPS = 4
        HIDDEN = 64
        TOPK = 2
        TEMP = 1.0
        DIL = 2
        EPS = 1e-06

        def _conv2d(x, w, b, dil=1):
            out = lax.conv_general_dilated(x, w, window_strides=(1, 1), padding='SAME', rhs_dilation=(dil, dil), dimension_numbers=('NCHW', 'OIHW', 'NCHW'))
            return out + b[None, :, None, None]

        def _avgpool3x3(x):
            s = lax.reduce_window(x, 0.0, lax.add, (1, 1, 3, 3), (1, 1, 1, 1), 'SAME')
            return s / 9.0

        def _forward(x, gw1, gb1, gw2, gb2, sw, sb, k1, kb1, k2, kb2):
            g = jnp.mean(x, axis=(2, 3))
            h = jax.nn.relu(g @ gw1.T + gb1)
            glog = h @ gw2.T + gb2
            slog = jnp.einsum('bchw,nc->bnhw', x, sw) + sb[None, :, None, None]
            logits = (glog[:, :, None, None] + slog) / TEMP
            weights = jax.nn.softmax(logits, axis=1)
            wt = jnp.moveaxis(weights, 1, -1)
            _, idx = lax.top_k(wt, TOPK)
            mask = jnp.sum(jax.nn.one_hot(idx, N_OPS, dtype=wt.dtype), axis=-2)
            w = wt * mask
            denom = jnp.maximum(jnp.sum(w, axis=-1, keepdims=True), EPS)
            w = jnp.moveaxis(w / denom, -1, 1)
            out = x * w[:, 0:1]
            out = out + _conv2d(x, k1, kb1, 1) * w[:, 1:2]
            out = out + _conv2d(x, k2, kb2, DIL) * w[:, 2:3]
            out = out + _avgpool3x3(x) * w[:, 3:4]
            return out
        return _forward(x, gw1, gb1, gw2, gb2, sw, sb, k1, kb1, k2, kb2)

    def _L1_conv_ref(x, weight, bias):
        import jax, jax.numpy as jnp
        import numpy as np
        KERNEL = (3, 3)
        STRIDE = (1, 1)
        PADDING = ((1, 1), (1, 1))
        DILATION = (1, 1)
        out = jax.lax.conv_general_dilated(x, weight, window_strides=STRIDE, padding=PADDING, rhs_dilation=DILATION, dimension_numbers=('NCHW', 'OIHW', 'NCHW'), feature_group_count=1)
        return out + bias[None, :, None, None]

    def _gn(v, G=16, eps=1e-5):
        B_, C_, H_, W_ = v.shape
        g = v.reshape(B_, G, C_ // G, H_, W_)
        m = jnp.mean(g, axis=(2, 3, 4), keepdims=True)
        s = jnp.var(g, axis=(2, 3, 4), keepdims=True)
        return ((g - m) / jnp.sqrt(s + eps)).reshape(v.shape)

    def _ln_c(v, eps=1e-6):
        m = jnp.mean(v, axis=1, keepdims=True)
        s = jnp.var(v, axis=1, keepdims=True)
        return (v - m) / jnp.sqrt(s + eps)

    def _ln_t(v, eps=1e-5):
        m = jnp.mean(v, axis=-1, keepdims=True)
        s = jnp.var(v, axis=-1, keepdims=True)
        return (v - m) / jnp.sqrt(s + eps)

    def _to_tokens(v):
        B_, C_, H_, W_ = v.shape
        return v.reshape(B_, C_, H_ * W_).transpose(0, 2, 1)
    def _from_tokens(t, like):
        B_, C_, H_, W_ = like.shape
        return t.transpose(0, 2, 1).reshape(B_, C_, H_, W_)

    x = x + _L0_conv_ref(_gn(x), L0_conv_gw1, L0_conv_gb1, L0_conv_gw2, L0_conv_gb2, L0_conv_sw, L0_conv_sb, L0_conv_k1, L0_conv_kb1, L0_conv_k2, L0_conv_kb2)
    x = x + _L1_conv_ref(_gn(x), L1_conv_weight, L1_conv_bias)
    return x


_drawn_inputs = setup_inputs


def setup_inputs(seed=0):
    import zlib

    import numpy as np

    out = dict(_drawn_inputs(seed))
    spreads = {'L0_conv_gb1': (0.0, 0.1),
     'L0_conv_gb2': (0.0, 0.1),
     'L0_conv_sb': (0.0, 0.1),
     'L0_conv_kb1': (0.0, 0.346),
     'L0_conv_kb2': (0.0, 0.32)}
    factors = {'L0_conv_gw1': 7.263}
    for name, (base, spread) in spreads.items():
        noise = np.random.default_rng([zlib.crc32(name.encode()), seed]).standard_normal(out[name].shape)
        drawn = base * np.exp(spread * noise) if base else spread * noise
        out[name] = jnp.asarray(drawn.astype(out[name].dtype))
    for name, factor in factors.items():
        out[name] = (out[name] * factor).astype(out[name].dtype)
    return out
```

```python
from contextlib import ExitStack

import numpy as np

import concourse.bass as bass
from concourse import mybir

F32 = mybir.dt.float32
F16 = mybir.dt.float16
ALU = mybir.AluOpType
ACT = mybir.ActivationFunctionType

P = 128
C = 32
B4 = P // C
N_OPS = 4
QU = 4
QT = 2
TU = QU // QT
PADW = 2
CENTRE, HALO, UPPER, LOWER = range(4)
HI, LO = 0, 1
X_SCALE = 16.0
W_SCALE = 32.0
PROB_SCALE = 1024.0
PRODUCTS = ((HI, HI), (LO, HI), (HI, LO))
GN_EPS = 1e-5


def vertical_taps():
    return [(k, b, k - b) for k in range(B4) for b in range(2) if 0 <= k - b <= 2]


def dilated_centre_taps():
    return [(k, b, (k - b) // 2 + 1) for k in range(B4) for b in range(B4) if (k - b) in (-2, 0, 2)]


def dilated_halo_taps():
    return [(k, k, 0 if k < 2 else 2) for k in range(B4)]


def build(nc, x, gw1t, gb1, gw2t, gb2, sb_, swt, k1t, kb1, k2t, kb2, l1t, l1b, avg, ident, select, vpool, out):
    NS, _, NQ, W = x.shape
    NU = NQ // QU
    NI = NU // 2
    NT = NU * TU
    HID = gw1t.shape[1]
    WP = W + 2 * PADW
    HALVES = W // P
    XCOLS = HALVES * QU * B4
    TF = QT * W
    FULL_COPIES, CONV_COPIES = 7, 4

    with ExitStack() as ctx:
        def sb(name, shape, dt=F32):
            return ctx.enter_context(nc.sbuf_tensor(name, shape, dt))

        def pb(name, shape, dt=F32):
            return ctx.enter_context(nc.psum_tensor(name, shape, dt))

        def sem(name):
            return ctx.enter_context(nc.semaphore(name))

        image = sb("image", [P, NQ, W])
        norm = sb("norm", [P, NQ + 2, 2, WP], F16)
        wins = [sb(f"wins{j}", [P, 4, QU, 2, WP], F16) for j in range(2)]
        router_w = [sb(f"router_w{n}", [P, QT, W]) for n in range(N_OPS)]
        xn = [sb(f"xn{t}", [P, QT, W]) for t in range(2)]
        vsum = sb("vsum", [P, QT, W + 2])
        pool_p = [sb(f"pool_p{t}", [P, QT, W]) for t in range(2)]
        base = [sb(f"base{t}", [P, QT, W]) for t in range(2)]
        prod = sb("prod", [P, QT, W])
        scaled = sb("scaled", [P, QT, W])
        w_v1 = sb("w_v1", [P, 3, 2, 2 * C], F16)
        w_l1 = sb("w_l1", [P, 3, 2, 2 * C], F16)
        w_dc = sb("w_dc", [P, 3, 2, P], F16)
        w_dh = sb("w_dh", [P, 3, 2, P], F16)
        w_sw = sb("w_sw", [P, 2, B4 * N_OPS], F16)
        w_pool = sb("w_pool", [P, 2 * C], F16)
        sel = sb("sel", [P, QU, N_OPS, P], F16)
        idn = sb("idn", [P, P], F16)
        avg_sb = sb("avg_sb", [P, P])
        gw1_sb = sb("gw1_sb", [P, HID])
        gb1_sb = sb("gb1_sb", [HID, 1])
        gw2_sb = sb("gw2_sb", [HID, N_OPS])
        gb2_sb = sb("gb2_sb", [P, N_OPS])
        sb_sb = sb("sb_sb", [P, N_OPS])
        biases = sb("biases", [P, 3])
        kbs = sb("kbs", [P, 2])
        bst = sb("bst", [P, NT, 6])
        mv = sb("mv", [P, 2])
        st = sb("st", [P, 16])
        D_, V2, VE, SD, R_, T1, T2, GN_, MG = (st[:, k:k + 1] for k in range(9))
        coef = [sb(f"coef{k}", [P, 4]) for k in range(2)]
        hid = sb("hid", [HID, 1])
        hid_rep = sb("hid_rep", [HID, P])
        rbias = sb("rbias", [P, N_OPS])
        logit = sb("logit", [P, N_OPS, XCOLS])
        beats1 = sb("beats1", [P, N_OPS + 1, XCOLS])
        beats2 = sb("beats2", [P, N_OPS + 2, XCOLS])
        beats3 = sb("beats3", [P, N_OPS + 3, XCOLS])
        diff1 = sb("diff1", [P, N_OPS, XCOLS])
        diff2 = sb("diff2", [P, N_OPS, XCOLS])
        top = sb("top", [P, 2, XCOLS])
        expo = sb("expo", [P, N_OPS, XCOLS])
        rden = sb("rden", [P, XCOLS])
        w_px = sb("w_px", [P, 2, QU, N_OPS, B4 * HALVES], F16)
        w_row = sb("w_row", [P, W], F16)

        p_v1 = [pb(f"p_v1_{t}", [P, QT, W]) for t in range(2)]
        p_dil = [pb(f"p_dil_{t}", [P, QT, W]) for t in range(2)]
        p_pool = pb("p_pool", [P, QT, W])
        p_w = [pb(f"p_w{j}", [P, QT, W]) for j in range(2)]
        p_misc = pb("p_misc", [P, 512])
        p_logit = p_misc[:, 0:XCOLS * N_OPS].rearrange("p (x n) -> p x n", n=N_OPS)
        p_logit_qh = p_misc[:, 0:XCOLS * N_OPS].rearrange("p (q b h n) -> p q h b n", q=QU, b=B4, n=N_OPS)
        p_stat = p_misc[:, 160:176]
        p_tr = p_misc[:, 256:256 + W // 2].bitcast(F16)

        consts_in = sem("consts_in")
        stage_zero = sem("stage_zero")
        taps_in = sem("taps_in")
        split_w = sem("split_w")
        gate_ready = sem("gate_ready")
        set_up = sem("set_up")
        init_step = sem("init_step")
        x_in = sem("x_in")
        wins_in = [sem(f"wins_in{j}") for j in range(2)]
        out_st = [sem(f"out_st{t}") for t in range(2)]
        stats_step = sem("stats_step")
        mean_in = sem("mean_in")
        stat_sum = sem("stat_sum")
        sq_in = sem("sq_in")
        sq_done = sem("sq_done")
        hid_done = sem("hid_done")
        coef_ready = sem("coef_ready")
        bst_step = sem("bst_step")
        split_step = sem("split_step")
        hi_ready = sem("hi_ready")
        lo_ready = sem("lo_ready")
        logits_ready = sem("logits_ready")
        router_step = sem("router_step")
        exp_in = sem("exp_in")
        exp_done = sem("exp_done")
        probs_ready = sem("probs_ready")
        tr_ready = sem("tr_ready")
        w_row_ready = sem("w_row_ready")
        pool_psum = sem("pool_psum")
        vsum_ready = sem("vsum_ready")
        hsum_step = sem("hsum_step")
        pw_ready = sem("pw_ready")
        router_w_ready = sem("router_w_ready")
        xn_ready = sem("xn_ready")
        w0_used = sem("w0_used")
        base_step = sem("base_step")
        base_ready = sem("base_ready")
        pool_ready = sem("pool_ready")
        v1_psum = sem("v1_psum")
        dil_psum = sem("dil_psum")
        conv_free = sem("conv_free")
        comb_step = sem("comb_step")
        comb_done = sem("comb_done")
        l1_psum = sem("l1_psum")
        l1_evac = sem("l1_evac")
        out_ready = sem("out_ready")

        flat = wins[0][:].rearrange("p a q h w -> p (a q h w)").bitcast(F32)
        widths = (3 * 2 * C, 3 * 2 * C, 3 * P, 3 * P, B4 * N_OPS)
        starts = [sum(widths[:k]) for k in range(len(widths) + 1)]
        stage_v1, stage_l1, stage_dc, stage_dh = (
            flat[:, starts[k]:starts[k + 1]].rearrange("p (a m) -> p a m", a=3) for k in range(4))
        stage_sw = flat[:, starts[4]:starts[5]]
        STAGED = [(stage_v1, [w_v1[:, :, p_, :] for p_ in (HI, LO)]), (stage_l1, [w_l1[:, :, p_, :] for p_ in (HI, LO)]),
                  (stage_dc, [w_dc[:, :, p_, :] for p_ in (HI, LO)]), (stage_dh, [w_dh[:, :, p_, :] for p_ in (HI, LO)]),
                  (stage_sw, [w_sw[:, p_, :] for p_ in (HI, LO)])]
        N_TAPS = 2 * len(vertical_taps()) + len(dilated_centre_taps()) + len(dilated_halo_taps()) + B4

        small = [(avg_sb[:], avg), (idn[:], ident), (sel[:].rearrange("p q n m -> p (q n m)"), select),
                 (w_pool[:], vpool), (gb1_sb[:], gb1), (gw2_sb[:], gw2t), (gb2_sb[:], gb2), (sb_sb[:], sb_),
                 (biases[:, 0:1], kb1), (biases[:, 1:2], kb2), (biases[:, 2:3], l1b)]
        small += [(gw1_sb[C * b:C * b + C, :], gw1t) for b in range(B4)]

        block = ctx.enter_context(nc.Block())

        def unit(n, u):
            return n * NU + u

        def tile(n, u, t):
            return n * NT + u * TU + t

        def wins_count(n, layer, i):
            per_image = NI * 16 * (FULL_COPIES + CONV_COPIES)
            return 16 + n * per_image + (layer * NI * FULL_COPIES + i * (CONV_COPIES if layer else FULL_COPIES)) * 16

        def steps(eng, body, first, last):
            if last - first == 1:
                body(first)
            elif last > first:
                with eng.Fori(first, last) as i:
                    body(i)

        def images(eng, body):
            if NS > 2:
                with eng.Fori(0, NS - 1) as n:
                    body(n, False)
            elif NS == 2:
                body(0, False)
            body(NS - 1, True)

        def held(eng, count):
            if not isinstance(count, int):
                eng.compute_val(count)
            return count

        def q_tile(u, t):
            return bass.ds(u * QU + t * QT, QT)

        class Order:

            def __init__(self, eng, s, calls, per):
                self.eng, self.s, self.start, self.per, self.k = eng, s, calls * per, per, 0

            def mark(self, ins):
                self.k += 1
                return ins.then_inc(self.s, 1)

            def wait(self):
                self.eng.wait_ge(self.s, self.start + self.k)

            def close(self):
                assert self.k == self.per, (self.k, self.per)

        @block.sync
        def _(sp):
            def load_x(n, i):
                q = bass.ds(i * 2 * QU, 2 * QU)
                sp.dma_start(image[:, q, :], x[n, :, q, :] if isinstance(n, int) else
                             x[bass.ds(n, 1), :, q, :].rearrange("a p q w -> (a p) q w")).then_inc(x_in, 16)

            for j in range(2):
                sp.sem_inc(wins_in[j], 16)
            for dst, src in small:
                sp.dma_start(dst, src).then_inc(consts_in, 16)
            sp.wait_ge(stage_zero, 1)
            for k, b, kh in vertical_taps():
                rows, cols = slice(C * k, C * k + C), slice(C * b, C * b + C)
                sp.dma_start(stage_v1[rows, :, cols], k1t[:, kh, :, :]).then_inc(taps_in, 16)
                sp.dma_start(stage_l1[rows, :, cols], l1t[:, kh, :, :]).then_inc(taps_in, 16)
            for stage, taps in ((stage_dc, dilated_centre_taps()), (stage_dh, dilated_halo_taps())):
                for k, b, kh in taps:
                    sp.dma_start(stage[C * k:C * k + C, :, C * b:C * b + C], k2t[:, kh, :, :]).then_inc(taps_in, 16)
            for b in range(B4):
                sp.dma_start(stage_sw[C * b:C * b + C, N_OPS * b:N_OPS * b + N_OPS], swt).then_inc(taps_in, 16)
            for i in range(NI):
                if i:
                    sp.wait_ge(x_in, 16 * i)
                load_x(0, i)
            sp.wait_ge(set_up, 1)

            def window_copies(n, layer, i, j, end):
                u = 2 * i + j
                split = held(sp, n * 2 * NT + layer * NT + (NT if end else (u + 2) * TU))
                lo_split = held(sp, n * 2 * NT + layer * NT + (NT if end else (u + 2) * TU) + 1)
                dil_done = held(sp, 3 + (n + 1) * NT if layer else 1 + tile(n, u, 0))
                l1_done = held(sp, 1 + tile(n, u, 0) if layer else 3 + n * NT)
                sp.wait_ge(dil_psum, dil_done)
                sp.wait_ge(l1_psum, l1_done)
                sp.wait_ge(hi_ready, split)
                sp.wait_ge(lo_ready, lo_split)
                before, here, after = (bass.ds(u * QU + d, QU) for d in range(3))

                def copy(kind, dst, src, q):
                    sp.dma_start(wins[j][dst, kind, :, :, :], norm[src, q, :, :]).then_inc(wins_in[j], 16)

                if layer == 0:
                    copy(CENTRE, slice(0, P), slice(0, P), here)
                copy(UPPER, slice(0, C), slice(3 * C, P), before)
                copy(UPPER, slice(C, P), slice(0, 3 * C), here)
                copy(LOWER, slice(0, 3 * C), slice(C, P), here)
                copy(LOWER, slice(3 * C, P), slice(0, C), after)
                if layer == 0:
                    copy(HALO, slice(0, 2 * C), slice(2 * C, P), before)
                    copy(HALO, slice(2 * C, P), slice(0, 2 * C), after)

            def image_body(n, last):
                def step0(i, end=False):
                    window_copies(n, 0, i, 0, False)
                    window_copies(n, 0, i, 1, end)

                steps(sp, step0, 0, NI - 1)
                step0(NI - 1, True)

                def step1(i, first=False, end=False):
                    window_copies(n, 1, i, 0, False)
                    window_copies(n, 1, i, 1, end)
                    if not first and not last:
                        next_x(i - 1)

                def next_x(i):
                    outputs_made = held(sp, 2 + tile(n, 2 * i + 2, 0))
                    loaded = held(sp, (n * NI + i + NI) * 16)
                    sp.wait_ge(out_ready, outputs_made)
                    sp.wait_ge(x_in, loaded)
                    load_x(n + 1, i)

                step1(0, first=True)
                steps(sp, step1, 1, NI - 1)
                step1(NI - 1, end=True)
                if not last:
                    next_x(NI - 1)

            images(sp, image_body)

        @block.vector
        def _(dve):
            for s_, k in ((conv_free, 2), (comb_done, 2), (lo_ready, 1)):
                dve.sem_inc(s_, k)
            nc.vector.memset(flat[:, 0:starts[-1]], 0.0).then_inc(stage_zero, 1)
            init = Order(dve, init_step, 0, 22)
            init.mark(nc.vector.memset(norm[:, 0, :, :], 0.0))
            init.mark(nc.vector.memset(norm[:, NQ + 1, :, :], 0.0))
            init.mark(nc.vector.memset(norm[:, 1:NQ + 1, :, 0:PADW], 0.0))
            init.mark(nc.vector.memset(norm[:, 1:NQ + 1, :, PADW + W:WP], 0.0))
            init.mark(nc.vector.memset(vsum[:, :, 0:1], 0.0))
            init.mark(nc.vector.memset(vsum[:, :, W + 1:W + 2], 0.0))
            init.mark(nc.vector.memset(beats1[:], 0.0))
            init.mark(nc.vector.memset(beats2[:], 0.0))
            for m, v in enumerate((2.0, 0.0, 0.0, 0.0, -1.0, 0.0, 1.0)):
                init.mark(nc.vector.memset(beats3[:, m, :], v))
            dve.wait_ge(taps_in, 16 * N_TAPS)
            dve.wait_ge(consts_in, 16 * len(small))
            for src, _ in STAGED:
                init.mark(nc.vector.tensor_scalar(src, src, W_SCALE, None, ALU.mult))
            init.wait()
            for src, dst in STAGED:
                nc.vector.tensor_copy(dst[HI], src).then_inc(split_w, 1)
            dve.wait_ge(split_w, len(STAGED))
            for src, dst in STAGED:
                nc.vector.tensor_tensor(dst[LO], src, dst[HI], ALU.subtract).then_inc(split_w, 1)
            init.mark(nc.vector.tensor_scalar(kbs[:], biases[:, 0:2], X_SCALE * W_SCALE, None, ALU.mult))
            init.mark(nc.vector.tensor_tensor(sb_sb[:], sb_sb[:], gb2_sb[:], ALU.add))
            dve.wait_ge(split_w, 2 * len(STAGED))
            init.wait()
            nc.vector.memset(rden[:], 0.0).then_inc(set_up, 1)
            init.close()

            def tile_stats(u, t):
                nc.vector.bn_stats(bst[:, bass.ds(u * TU + t, 1), :].rearrange("p a s -> p (a s)"),
                                   image[:, q_tile(u, t), :].rearrange("p q w -> p (q w)")).then_inc(bst_step, 1)

            def x_stats(n, i):
                dve.wait_ge(x_in, (n * NI + i + 1) * 16)
                for j in range(2):
                    for t in range(TU):
                        tile_stats(2 * i + j, t)

            def finish_stats(n, layer):
                s = Order(dve, stats_step, n * 2 + layer, 8)
                dve.wait_ge(bst_step, n * 2 * NT + layer * NT + NT)
                c = coef[layer]
                nc.vector.memset(T1, 0.0)
                nc.vector.bn_aggr(mv[:], bst[:].rearrange("p a s -> p (a s)")).then_inc(mean_in, 1)
                dve.wait_ge(mean_in, n * 2 + layer + 1)
                dve.wait_ge(stat_sum, n * 6 + layer * 4 + 1)
                s.mark(nc.vector.tensor_copy(MG, p_stat[:, 0:1]))
                s.wait()
                s.mark(nc.vector.tensor_tensor(D_, mv[:, 0:1], MG, ALU.subtract))
                s.wait()
                nc.vector.scalar_tensor_tensor(V2, D_, D_, mv[:, 1:2], ALU.mult, ALU.add).then_inc(sq_in, 1)
                dve.wait_ge(stat_sum, n * 6 + layer * 4 + 2)
                nc.vector.tensor_scalar(VE, p_stat[:, 1:2], GN_EPS, None, ALU.add).then_inc(sq_in, 1)
                dve.wait_ge(sq_done, n * 2 + layer + 1)
                s.mark(nc.vector.reciprocal(R_, SD))
                s.wait()
                s.mark(nc.vector.scalar_tensor_tensor(T1, R_, R_, VE, ALU.mult, ALU.mult))
                s.wait()
                s.mark(nc.vector.tensor_scalar(T2, T1, -0.5, 1.5, ALU.mult, ALU.add))
                s.wait()
                s.mark(nc.vector.tensor_tensor(c[:, 0:1], R_, T2, ALU.mult))
                s.wait()
                s.mark(nc.vector.scalar_tensor_tensor(c[:, 1:2], MG, -1.0, c[:, 0:1], ALU.mult, ALU.mult))
                s.mark(nc.vector.tensor_tensor(GN_, D_, c[:, 0:1], ALU.mult))
                s.wait()
                nc.vector.tensor_scalar(c[:, 2:4], c[:, 0:2], X_SCALE, None, ALU.mult).then_inc(coef_ready, 1)
                s.close()

            def gate(n):
                dve.wait_ge(hid_done, n + 1)
                nc.vector.tensor_copy(hid_rep[:], hid[:].to_broadcast([HID, P])).then_inc(sq_in, 1)
                dve.wait_ge(stat_sum, n * 6 + 4)
                nc.vector.tensor_tensor(rbias[:], p_stat[:, 4:8], sb_sb[:], ALU.add).then_inc(gate_ready, 1)

            def split_unit(n, layer, u):
                c = coef[layer]
                for t in range(TU):
                    k = n * 2 * NT + layer * NT + u * TU + t
                    src = image[:, q_tile(u, t), :]
                    dst = norm[:, bass.ds(u * QU + t * QT + 1, QT), :, PADW:PADW + W]
                    dve.wait_ge(lo_ready, 1 + k)
                    nc.vector.tensor_scalar(scaled[:], src, c[:, 2:3], c[:, 3:4], ALU.mult,
                                            ALU.add).then_inc(split_step, 1)
                    dve.wait_ge(split_step, k + 1)
                    dve.wait_ge(hi_ready, k + 1)
                    nc.vector.tensor_tensor(dst[:, :, LO, :], scaled[:], dst[:, :, HI, :],
                                            ALU.subtract).then_inc(lo_ready, 1)

            def router(n, u):
                k = unit(n, u)
                s = Order(dve, router_step, k, 17)
                dve.wait_ge(logits_ready, k + 1)
                bias = rbias[:].rearrange("p (n o) -> p n o", o=1).to_broadcast([P, N_OPS, XCOLS])
                s.mark(nc.vector.scalar_tensor_tensor(logit[:], p_logit.rearrange("p x n -> p n x"),
                                                      1.0 / (X_SCALE * W_SCALE), bias, ALU.mult, ALU.add))
                s.wait()
                for d, g in ((1, beats1), (2, beats2), (3, beats3)):
                    s.mark(nc.vector.tensor_tensor(g[:, d:N_OPS, :], logit[:, 0:N_OPS - d, :],
                                                   logit[:, d:N_OPS, :], ALU.is_ge))
                s.mark(nc.vector.tensor_tensor(top[:], logit[:, 0:2, :], logit[:, 2:4, :], ALU.max))
                s.wait()
                s.mark(nc.vector.tensor_tensor(diff1[:], beats1[:, 1:N_OPS + 1, :], beats1[:, 0:N_OPS, :],
                                               ALU.subtract))
                s.mark(nc.vector.tensor_tensor(diff2[:], beats2[:, 2:N_OPS + 2, :], beats2[:, 0:N_OPS, :],
                                               ALU.subtract))
                s.mark(nc.vector.tensor_tensor(top[:, 0, :], top[:, 0, :], top[:, 1, :], ALU.max))
                s.wait()
                s.mark(nc.vector.tensor_tensor(diff1[:], diff1[:], diff2[:], ALU.add))
                peak = top[:, 0:1, :].to_broadcast([P, N_OPS, XCOLS])
                nc.vector.tensor_tensor(logit[:], logit[:], peak, ALU.subtract).then_inc(exp_in, 1)
                s.wait()
                s.mark(nc.vector.tensor_tensor(diff2[:], beats3[:, 3:N_OPS + 3, :], beats3[:, 0:N_OPS, :],
                                               ALU.subtract))
                s.wait()
                s.mark(nc.vector.tensor_tensor(diff1[:], diff1[:], diff2[:], ALU.add))
                s.wait()
                dve.wait_ge(exp_done, k + 1)
                s.mark(nc.vector.scalar_tensor_tensor(expo[:], diff1[:], 0.0, expo[:], ALU.is_ge, ALU.mult))
                s.wait()
                s.mark(nc.vector.tensor_tensor(top[:], expo[:, 0:2, :], expo[:, 2:4, :], ALU.add))
                s.wait()
                s.mark(nc.vector.tensor_tensor(top[:, 0, :], top[:, 0, :], top[:, 1, :], ALU.add))
                s.wait()
                s.mark(nc.vector.reciprocal(rden[:], top[:, 0, :]))
                s.wait()
                recip = rden[:].rearrange("p (o x) -> p o x", o=1).to_broadcast([P, N_OPS, XCOLS])
                s.mark(nc.vector.scalar_tensor_tensor(logit[:], expo[:], PROB_SCALE, recip, ALU.mult, ALU.mult))
                s.wait()
                lg = logit[:].rearrange("p n (q b) -> p n q b", q=QU)
                px = w_px[:].rearrange("p a q n b -> p a n q b")
                s.mark(nc.vector.tensor_copy(px[:, HI], lg))
                s.wait()
                nc.vector.tensor_tensor(px[:, LO], lg, px[:, HI], ALU.subtract).then_inc(probs_ready, 1)
                s.close()

            def combine(n, u, t):
                k = tile(n, u, t)
                s = Order(dve, comb_step, k, 3)
                dst = image[:, q_tile(u, t), :]
                dve.wait_ge(v1_psum, k + 1)
                dve.wait_ge(router_w_ready, 2 + 4 * k + 2)
                dve.wait_ge(comb_done, 2 + k)
                s.mark(nc.vector.scalar_tensor_tensor(prod[:], p_v1[t][:], kbs[:, 0:1], router_w[1][:],
                                                      ALU.add, ALU.mult))
                dve.wait_ge(dil_psum, 3 + k + 1)
                dve.wait_ge(router_w_ready, 2 + 4 * k + 3)
                nc.vector.scalar_tensor_tensor(router_w[2][:], p_dil[t][:], kbs[:, 1:2], router_w[2][:],
                                               ALU.add, ALU.mult).then_inc(conv_free, 1)
                dve.wait_ge(conv_free, 2 + k + 1)
                s.wait()
                s.mark(nc.vector.tensor_tensor(prod[:], prod[:], router_w[2][:], ALU.add))
                dve.wait_ge(pool_ready, 1 + k + 1)
                s.wait()
                s.mark(nc.vector.tensor_tensor(prod[:], prod[:], pool_p[t][:], ALU.add))
                dve.wait_ge(base_ready, k + 1)
                s.wait()
                nc.vector.tensor_tensor(dst, prod[:], base[t][:], ALU.add).then_inc(comb_done, 1)
                dve.wait_ge(comb_done, 2 + k + 1)
                tile_stats(u, t)
                s.close()

            def image_body(n, last):
                finish_stats(n, 0)
                dve.wait_ge(coef_ready, 2 * n + 1)
                dve.wait_ge(wins_in[0], wins_count(n, 0, 0))
                dve.wait_ge(wins_in[1], wins_count(n, 0, 0))
                split_unit(n, 0, 0)
                split_unit(n, 0, 1)
                gate(n)
                dve.wait_ge(gate_ready, n + 1)
                router(n, 0)

                def step0(i, end=False):
                    for j in range(2):
                        u = 2 * i + j
                        if not end:
                            split_unit(n, 0, u + 2)
                        combine(n, u, 0)
                        if not (end and j == 1):
                            router(n, u + 1)
                        combine(n, u, 1)

                steps(dve, step0, 0, NI - 1)
                step0(NI - 1, True)

                finish_stats(n, 1)
                dve.wait_ge(coef_ready, 2 * n + 2)
                dve.wait_ge(wins_in[0], wins_count(n, 1, 0))
                dve.wait_ge(wins_in[1], wins_count(n, 1, 0))
                split_unit(n, 1, 0)
                split_unit(n, 1, 1)

                def step1(i, first=False, end=False):
                    if not end:
                        split_unit(n, 1, 2 * i + 2)
                        split_unit(n, 1, 2 * i + 3)
                    if not first and not last:
                        x_stats(n + 1, i - 1)

                step1(0, first=True)
                steps(dve, step1, 1, NI - 1)
                step1(NI - 1, end=True)
                if not last:
                    x_stats(n + 1, NI - 1)

            steps(dve, lambda i: x_stats(0, i), 0, NI)
            images(dve, image_body)

        @block.scalar
        def _(act):
            for s_, k in ((router_w_ready, 2), (l1_evac, 2), (vsum_ready, 1), (out_st[0], 16), (out_st[1], 16)):
                act.sem_inc(s_, k)
            act.wait_ge(set_up, 1)

            def stats_root(n, layer):
                act.wait_ge(sq_in, n * 5 + layer * 3 + 2)
                nc.scalar.activation(SD, VE, ACT.Sqrt).then_inc(sq_done, 1)

            def hi_unit(n, layer, u):
                c = coef[layer]
                for t in range(TU):
                    nc.scalar.activation(norm[:, bass.ds(u * QU + t * QT + 1, QT), HI, PADW:PADW + W],
                                         image[:, q_tile(u, t), :], ACT.Identity, bias=c[:, 3:4],
                                         scale=c[:, 2:3]).then_inc(hi_ready, 1)

            def exps(n, u):
                act.wait_ge(exp_in, unit(n, u) + 1)
                nc.scalar.activation(expo[:], logit[:], ACT.Exp).then_inc(exp_done, 1)

            def weights_row(n, u):
                act.wait_ge(tr_ready, unit(n, u) + 1)
                nc.scalar.copy(w_row[:], p_tr).then_inc(w_row_ready, 1)

            UNSCALE = [1.0 / PROB_SCALE, 1.0 / (PROB_SCALE * X_SCALE * W_SCALE),
                       1.0 / (PROB_SCALE * X_SCALE * W_SCALE), 1.0 / (PROB_SCALE * X_SCALE * 9.0)]

            def evacuate(n, u, t):
                k = tile(n, u, t)
                act.wait_ge(w0_used, 1 + k)
                nc.scalar.activation(xn[t][:], image[:, q_tile(u, t), :], ACT.Identity, bias=coef[0][:, 1:2],
                                     scale=coef[0][:, 0:1]).then_inc(xn_ready, 1)
                act.wait_ge(pool_psum, k + 1)
                act.wait_ge(hsum_step, 2 * k + 2)
                nc.scalar.copy(vsum[:, :, 1:1 + W], p_pool[:]).then_inc(vsum_ready, 1)
                for m in range(N_OPS):
                    act.wait_ge(pw_ready, 4 * k + m + 1)
                    if m == 0:
                        act.wait_ge(w0_used, 2 + k)
                    elif m == 3:
                        act.wait_ge(pool_ready, k + 1)
                    elif m == 1:
                        act.wait_ge(conv_free, k + 2)
                    elif m == 2:
                        act.wait_ge(comb_done, k + 2)
                    nc.scalar.activation(router_w[m][:], p_w[m % 2][:], ACT.Copy,
                                         scale=UNSCALE[m]).then_inc(router_w_ready, 1)

            def conv_out(n, u, t):
                k = tile(n, u, t)
                act.wait_ge(l1_psum, 3 + k + 1)
                act.wait_ge(out_ready, k + 1)
                nc.scalar.activation(xn[t][:], p_v1[t][:], ACT.Identity, bias=biases[:, 2:3],
                                     scale=1.0 / (X_SCALE * W_SCALE)).then_inc(l1_evac, 1)

            def store(n, u, t):
                act.wait_ge(out_ready, 2 + tile(n, u, t) + 1)
                q = q_tile(u, t)
                act.dma_start(out[n, :, q, :] if isinstance(n, int) else
                              out[bass.ds(n, 1), :, q, :].rearrange("a p q w -> (a p) q w"),
                              router_w[t][:]).then_inc(out_st[t], 16)

            def image_body(n, last):
                stats_root(n, 0)
                act.wait_ge(stat_sum, n * 6 + 3)
                nc.scalar.activation(hid[:], p_stat[0:HID, 2:3], ACT.Relu, bias=gb1_sb[:],
                                     scale=1.0 / B4).then_inc(hid_done, 1)
                act.wait_ge(coef_ready, 2 * n + 1)
                act.wait_ge(wins_in[0], wins_count(n, 0, 0))
                act.wait_ge(wins_in[1], wins_count(n, 0, 0))
                act.wait_ge(out_st[0], 16 + unit(n, 0) * 16)
                act.wait_ge(out_st[1], 16 + unit(n, 0) * 16)
                hi_unit(n, 0, 0)
                hi_unit(n, 0, 1)
                exps(n, 0)
                weights_row(n, 0)

                def step0(i, end=False):
                    for j in range(2):
                        u = 2 * i + j
                        if not end:
                            hi_unit(n, 0, u + 2)
                        evacuate(n, u, 0)
                        if not (end and j == 1):
                            exps(n, u + 1)
                        evacuate(n, u, 1)
                        if not (end and j == 1):
                            weights_row(n, u + 1)

                steps(act, step0, 0, NI - 1)
                step0(NI - 1, True)

                stats_root(n, 1)
                act.wait_ge(coef_ready, 2 * n + 2)
                act.wait_ge(wins_in[0], wins_count(n, 1, 0))
                act.wait_ge(wins_in[1], wins_count(n, 1, 0))
                hi_unit(n, 1, 0)
                hi_unit(n, 1, 1)

                def step1(i, end=False):
                    for j in range(2):
                        u = 2 * i + j
                        if not end:
                            hi_unit(n, 1, u + 2)
                        conv_out(n, u, 0)
                        conv_out(n, u, 1)
                        store(n, u, 0)
                        store(n, u, 1)

                steps(act, step1, 0, NI - 1)
                step1(NI - 1, True)

            images(act, image_body)
            act.wait_ge(out_st[0], 16 + NS * NU * 16)
            act.wait_ge(out_st[1], 16 + NS * NU * 16)

        @block.gpsimd
        def _(pool):
            for s_, k in ((hsum_step, 2), (w0_used, 2), (pool_ready, 1), (out_ready, 2)):
                pool.sem_inc(s_, k)
            pool.wait_ge(set_up, 1)

            def base_and_pool(n, u, t):
                k = tile(n, u, t)
                pool.wait_ge(xn_ready, k + 1)
                pool.wait_ge(comb_done, k + 1)
                pool.wait_ge(vsum_ready, 1 + k + 1)
                nc.gpsimd.tensor_tensor(pool_p[t][:], vsum[:, :, 0:W], vsum[:, :, 1:1 + W], ALU.add).then_inc(hsum_step, 1)
                pool.wait_ge(hsum_step, 2 + 2 * k + 1)
                nc.gpsimd.tensor_tensor(pool_p[t][:], pool_p[t][:], vsum[:, :, 2:2 + W], ALU.add).then_inc(hsum_step, 1)
                pool.wait_ge(router_w_ready, 2 + 4 * k + 1)
                nc.gpsimd.tensor_tensor(base[t][:], xn[t][:], router_w[0][:], ALU.mult).then_inc(w0_used, 1)
                pool.wait_ge(w0_used, 2 + k + 1)
                nc.gpsimd.tensor_tensor(base[t][:], base[t][:], image[:, q_tile(u, t), :],
                                        ALU.add).then_inc(base_ready, 1)
                pool.wait_ge(router_w_ready, 2 + 4 * k + 4)
                pool.wait_ge(hsum_step, 2 + 2 * k + 2)
                nc.gpsimd.tensor_tensor(pool_p[t][:], pool_p[t][:], router_w[3][:], ALU.mult).then_inc(pool_ready, 1)

            def residual(n, u, t):
                k = tile(n, u, t)
                pool.wait_ge(l1_evac, 2 + k + 1)
                pool.wait_ge(out_st[t], 16 + unit(n, u) * 16)
                nc.gpsimd.tensor_tensor(router_w[t][:], xn[t][:], image[:, q_tile(u, t), :],
                                        ALU.add).then_inc(out_ready, 1)

            def image_body(n, last):
                def step0(i):
                    for j in range(2):
                        for t in range(TU):
                            base_and_pool(n, 2 * i + j, t)

                def step1(i):
                    for j in range(2):
                        for t in range(TU):
                            residual(n, 2 * i + j, t)

                steps(pool, step0, 0, NI)
                steps(pool, step1, 0, NI)

            images(pool, image_body)

        @block.tensor
        def _(pe):
            for s_ in (dil_psum, l1_psum):
                pe.sem_inc(s_, 3)
            pe.wait_ge(set_up, 1)
            mm = nc.tensor.matmul

            def moving(j, kind, t, part_, kw, dil):
                off = PADW + (kw - 1) * dil
                return wins[j][:, kind, t * QT:(t + 1) * QT, part_, off:off + W]

            def group_stats(n, layer):
                pe.wait_ge(mean_in, 2 * n + layer + 1)
                mm(p_stat[:, 0:1], avg_sb[:], mv[:, 0:1], start=True, stop=True).then_inc(stat_sum, 1)
                pe.wait_ge(sq_in, n * 5 + layer * 3 + 1)
                mm(p_stat[:, 1:2], avg_sb[:], V2, start=True, stop=True).then_inc(stat_sum, 1)

            def gate(n):
                pe.wait_ge(coef_ready, 2 * n + 1)
                mm(p_stat[0:HID, 2:3], gw1_sb[:], GN_, start=True, stop=True).then_inc(stat_sum, 1)
                pe.wait_ge(sq_in, n * 5 + 3)
                mm(p_stat[:, 4:8], hid_rep[:], gw2_sb[:], start=True, stop=True).then_inc(stat_sum, 1)

            def logits(n, u, j):
                for q in range(QU):
                    for h in range(HALVES):
                        for m, (xp, wp) in enumerate(PRODUCTS):
                            px = wins[j][:, CENTRE, q, xp, PADW + h * P:PADW + h * P + P]
                            last = mm(p_logit_qh[:, q, h], px, w_sw[:, wp, :],
                                      start=m == 0, stop=m == len(PRODUCTS) - 1)
                last.then_inc(logits_ready, 1)

            def transpose_weights(n, u):
                pe.wait_ge(probs_ready, unit(n, u) + 1)
                for h in range(HALVES):
                    src = w_px[:].rearrange("p a q n (b h) -> p h (a q n b)", h=HALVES)[:, h]
                    last = nc.tensor.transpose(p_tr[:, h * P:(h + 1) * P], src, idn[:])
                last.then_inc(tr_ready, 1)

            def vertical(dst, weights, j, t, parts):
                todo = [(kw, xp, wp) for kw in range(3) for xp, wp in parts]
                for m, (kw, xp, wp) in enumerate(todo):
                    for half, kind in enumerate((UPPER, LOWER)):
                        last = mm(dst[half * 2 * C:(half + 1) * 2 * C, :, :], weights[:, kw, wp, :],
                                  moving(j, kind, t, xp, kw, 1), start=m == 0, stop=m == len(todo) - 1)
                return last

            def op_weight(n, u, t, m):
                k = tile(n, u, t)
                pe.wait_ge(router_w_ready, 4 * k + m + 1)
                for g in range(QT):
                    last = mm(p_w[m % 2][:, g, :], sel[:, t * QT + g, m, :], w_row[:], start=True, stop=True)
                last.then_inc(pw_ready, 1)

            def layer0_tile(n, u, j, t):
                k = tile(n, u, t)
                pe.wait_ge(vsum_ready, 1 + k)
                for m, xp in enumerate((HI, LO)):
                    for half, kind in enumerate((UPPER, LOWER)):
                        last = mm(p_pool[half * 2 * C:(half + 1) * 2 * C, :, :], w_pool[:],
                                  moving(j, kind, t, xp, 1, 1), start=m == 0, stop=m == 1)
                last.then_inc(pool_psum, 1)
                pe.wait_ge(conv_free, k + 1)
                vertical(p_v1[t], w_v1, j, t, PRODUCTS).then_inc(v1_psum, 1)
                pe.wait_ge(w_row_ready, unit(n, u) + 1)
                op_weight(n, u, t, 0)
                op_weight(n, u, t, 1)
                todo = [(w, kind, kw, xp, wp) for w, kind in ((w_dc, CENTRE), (w_dh, HALO))
                        for kw in range(3) for xp, wp in PRODUCTS]
                for m, (w, kind, kw, xp, wp) in enumerate(todo):
                    if m == len(todo) // 2:
                        op_weight(n, u, t, 2)
                        op_weight(n, u, t, 3)
                    last = mm(p_dil[t][:], w[:, kw, wp, :], moving(j, kind, t, xp, kw, 2),
                              start=m == 0, stop=m == len(todo) - 1)
                last.then_inc(dil_psum, 1)
                return last

            def windows_in(n, layer, i, j):
                pe.wait_ge(wins_in[j], wins_count(n, layer, i + 1))

            def image_body(n, last_image):
                group_stats(n, 0)
                gate(n)
                windows_in(n, 0, 0, 0)
                pe.wait_ge(gate_ready, n + 1)
                logits(n, 0, 0)
                transpose_weights(n, 0)

                def step0(i, end=False):
                    for j in range(2):
                        u = 2 * i + j
                        layer0_tile(n, u, j, 0)
                        if not (end and j == 1):
                            windows_in(n, 0, i + j, 1 - j)
                            logits(n, u + 1, 1 - j)
                        layer0_tile(n, u, j, 1)
                        if not (end and j == 1):
                            transpose_weights(n, u + 1)

                steps(pe, step0, 0, NI - 1)
                step0(NI - 1, True)

                group_stats(n, 1)

                def step1(i):
                    for j in range(2):
                        u = 2 * i + j
                        windows_in(n, 1, i, j)
                        for t in range(TU):
                            k = tile(n, u, t)
                            pe.wait_ge(l1_evac, k + 1)
                            vertical(p_v1[t], w_l1, j, t, PRODUCTS).then_inc(l1_psum, 1)

                steps(pe, step1, 0, NI)

            images(pe, image_body)


def layout(inputs):
    x = np.asarray(inputs["x"])
    n, c, h, w = x.shape
    q = h // B4
    g = {k: np.asarray(v) for k, v in inputs.items()}
    taps = lambda a: np.ascontiguousarray(a.transpose(1, 2, 3, 0))
    per_partition = lambda a: np.ascontiguousarray(np.tile(a, B4)[:, None])
    everywhere = lambda a: np.ascontiguousarray(np.tile(a[None, :], (P, 1)))
    avg = np.zeros((P, P), np.float32)
    group = (np.arange(P) % C) // 2
    avg[group[:, None] == group[None, :]] = 1.0 / (2 * B4)
    ident = np.eye(P, dtype=np.float16)
    select = np.zeros((P, QU, N_OPS, P), np.float16)
    for part_ in range(2):
        for qq in range(QU):
            for op in range(N_OPS):
                for b in range(B4):
                    select[((part_ * QU + qq) * N_OPS + op) * B4 + b, qq, op, C * b:C * b + C] = 1
    vpool = np.zeros((P, 2 * C), np.float16)
    for k, b, _ in vertical_taps():
        vpool[C * k + np.arange(C), C * b + np.arange(C)] = 1
    return {
        "x": np.ascontiguousarray(x.reshape(n, c, q, B4, w).transpose(0, 3, 1, 2, 4)).reshape(n, P, q, w),
        "gw1t": np.ascontiguousarray(g["L0_conv_gw1"].T), "gb1": np.ascontiguousarray(g["L0_conv_gb1"][:, None]),
        "gw2t": np.ascontiguousarray(g["L0_conv_gw2"].T), "gb2": everywhere(g["L0_conv_gb2"]),
        "sb_": everywhere(g["L0_conv_sb"]), "swt": np.ascontiguousarray(g["L0_conv_sw"].T),
        "k1t": taps(g["L0_conv_k1"]), "kb1": per_partition(g["L0_conv_kb1"]),
        "k2t": taps(g["L0_conv_k2"]), "kb2": per_partition(g["L0_conv_kb2"]),
        "l1t": taps(g["L1_conv_weight"]), "l1b": per_partition(g["L1_conv_bias"]),
        "avg": avg, "ident": ident, "select": select.reshape(P, -1), "vpool": vpool,
    }


def kernel(**inputs):
    import concourse.bacc as _bacc
    from concourse.bass_utils import run_bass_kernel_spmd as _run

    nc = _bacc.Bacc("TRN2", target_bir_lowering=False, num_devices=1)
    arrays = layout(inputs)
    args = {k: nc.dram_tensor(f"in_{k}", a.shape, mybir.dt.from_np(a.dtype), kind="ExternalInput").ap()
            for k, a in arrays.items()}
    n, p, q, w = arrays["x"].shape
    out = nc.dram_tensor("out_y", (n, p, q, w), F32, kind="ExternalOutput").ap()
    build(nc, out=out, **args)
    r = _run(nc, [{f"in_{k}": a for k, a in arrays.items()}], core_ids=[0])
    y = r.results[0]["out_y"]
    return y.reshape(n, B4, C, q, w).transpose(0, 2, 3, 1, 4).reshape(n, C, q * B4, w)
```

```python
from contextlib import ExitStack

import numpy as np

import concourse.bass as bass
from concourse import mybir

F32 = mybir.dt.float32
F16 = mybir.dt.float16
ALU = mybir.AluOpType
ACT = mybir.ActivationFunctionType

P = 128
C = 32
B4 = P // C
N_OPS = 4
QU = 4
QT = 2
TU = QU // QT
LEAD = 4
PADW = 2
UPPER, LOWER, EVEN, ODD = range(4)
HI, LO = 0, 1
X_SCALE = 16.0
W_SCALE = 32.0
PROB_SCALE = 1024.0
PRODUCTS = ((HI, HI), (LO, HI), (HI, LO))
GN_EPS = 1e-5


def vertical_taps():
    return [(k, b, k - b) for k in range(B4) for b in range(2) if 0 <= k - b <= 2]


def build(nc, x, gw1t, gb1, gw2t, gb2, sb_, swt, k1t, kb1, k2t, kb2, l1t, l1b, avg, ident, select, vpool, out):
    NS, _, NQ, W = x.shape
    NU = NQ // QU
    NI = NU // 2
    NT = NU * TU
    HID = gw1t.shape[1]
    WP = W + 2 * PADW
    HALVES = W // P
    XCOLS = HALVES * QU * B4
    FULL_COPIES, CONV_COPIES = 12, 4

    with ExitStack() as ctx:
        def sb(name, shape, dt=F32):
            return ctx.enter_context(nc.sbuf_tensor(name, shape, dt))

        def pb(name, shape, dt=F32):
            return ctx.enter_context(nc.psum_tensor(name, shape, dt))

        def sem(name):
            return ctx.enter_context(nc.semaphore(name))

        image = sb("image", [P, NQ, W])
        norm = sb("norm", [P, NQ + 2, 2, WP], F16)
        wins = [sb(f"wins{j}", [P, 4, QU, 2, WP], F16) for j in range(2)]
        router_w = [sb(f"router_w{n}", [P, QT, W]) for n in range(N_OPS)]
        xn = [sb(f"xn{t}", [P, QT, W]) for t in range(2)]
        vsum = sb("vsum", [P, QT, W + 2])
        pool_p = [sb(f"pool_p{t}", [P, QT, W]) for t in range(2)]
        base = [sb(f"base{t}", [P, QT, W]) for t in range(2)]
        prod = sb("prod", [P, QT, W])
        scaled = sb("scaled", [P, QT, W])
        w_v1 = sb("w_v1", [P, 3, 2, 2 * C], F16)
        w_l1 = sb("w_l1", [P, 3, 2, 2 * C], F16)
        w_v2 = sb("w_v2", [P, 3, 2, 2 * C], F16)
        w_sw = sb("w_sw", [P, 2, B4 * N_OPS], F16)
        w_pool = sb("w_pool", [P, 2 * C], F16)
        sel = sb("sel", [P, QU, N_OPS, P], F16)
        idn = sb("idn", [P, P], F16)
        avg_sb = sb("avg_sb", [P, P])
        gw1_sb = sb("gw1_sb", [P, HID])
        gb1_sb = sb("gb1_sb", [HID, 1])
        gw2_sb = sb("gw2_sb", [HID, N_OPS])
        gb2_sb = sb("gb2_sb", [P, N_OPS])
        sb_sb = sb("sb_sb", [P, N_OPS])
        biases = sb("biases", [P, 3])
        kbs = sb("kbs", [P, 2])
        bst = sb("bst", [P, NT, 6])
        mv = sb("mv", [P, 2])
        st = sb("st", [P, 16])
        D_, V2, VE, SD, R_, T1, T2, GN_, MG = (st[:, k:k + 1] for k in range(9))
        coef = [sb(f"coef{k}", [P, 4]) for k in range(2)]
        hid = sb("hid", [HID, 1])
        hid_rep = sb("hid_rep", [HID, P])
        rbias = sb("rbias", [P, N_OPS])
        logit = sb("logit", [P, N_OPS, XCOLS])
        beats1 = sb("beats1", [P, N_OPS + 1, XCOLS])
        beats2 = sb("beats2", [P, N_OPS + 2, XCOLS])
        beats3 = sb("beats3", [P, N_OPS + 3, XCOLS])
        diff1 = sb("diff1", [P, N_OPS, XCOLS])
        diff2 = sb("diff2", [P, N_OPS, XCOLS])
        top = sb("top", [P, 2, XCOLS])
        expo = sb("expo", [P, N_OPS, XCOLS])
        rden = sb("rden", [P, XCOLS])
        w_px = sb("w_px", [P, 2, QU, N_OPS, B4 * HALVES], F16)
        w_row = sb("w_row", [P, W], F16)

        p_v1 = [pb(f"p_v1_{t}", [P, QT, W]) for t in range(2)]
        p_dil = [pb(f"p_dil_{t}", [P, QT, W]) for t in range(2)]
        p_pool = pb("p_pool", [P, QT, W])
        p_w = [pb(f"p_w{j}", [P, QT, W]) for j in range(2)]
        p_misc = pb("p_misc", [P, 512])
        p_logit = p_misc[:, 0:XCOLS * N_OPS].rearrange("p (x n) -> p x n", n=N_OPS)
        p_logit_qh = p_misc[:, 0:XCOLS * N_OPS].rearrange("p (q b h n) -> p q h b n", q=QU, b=B4, n=N_OPS)
        p_stat = p_misc[:, 160:176]
        p_tr = p_misc[:, 256:256 + W // 2].bitcast(F16)

        consts_in = sem("consts_in")
        stage_zero = sem("stage_zero")
        taps_in = sem("taps_in")
        split_w = sem("split_w")
        gate_ready = sem("gate_ready")
        set_up = sem("set_up")
        init_step = sem("init_step")
        x_in = sem("x_in")
        wins_in = [sem(f"wins_in{j}") for j in range(2)]
        out_st = [sem(f"out_st{t}") for t in range(2)]
        stats_step = sem("stats_step")
        mean_in = sem("mean_in")
        stat_sum = sem("stat_sum")
        sq_in = sem("sq_in")
        sq_done = sem("sq_done")
        hid_done = sem("hid_done")
        coef_ready = sem("coef_ready")
        bst_step = sem("bst_step")
        split_step = sem("split_step")
        hi_ready = sem("hi_ready")
        lo_ready = sem("lo_ready")
        logits_ready = sem("logits_ready")
        router_step = sem("router_step")
        exp_in = sem("exp_in")
        exp_done = sem("exp_done")
        probs_ready = sem("probs_ready")
        tr_ready = sem("tr_ready")
        w_row_ready = sem("w_row_ready")
        pool_psum = sem("pool_psum")
        vsum_ready = sem("vsum_ready")
        hsum_step = sem("hsum_step")
        pw_ready = sem("pw_ready")
        router_w_ready = sem("router_w_ready")
        xn_ready = sem("xn_ready")
        w0_used = sem("w0_used")
        base_step = sem("base_step")
        base_ready = sem("base_ready")
        pool_ready = sem("pool_ready")
        v1_psum = sem("v1_psum")
        dil_psum = sem("dil_psum")
        conv_free = sem("conv_free")
        comb_step = sem("comb_step")
        comb_done = sem("comb_done")
        l1_psum = sem("l1_psum")
        l1_evac = sem("l1_evac")
        out_ready = sem("out_ready")

        flat = wins[0][:].rearrange("p a q h w -> p (a q h w)").bitcast(F32)
        widths = (3 * 2 * C, 3 * 2 * C, 3 * 2 * C, B4 * N_OPS)
        starts = [sum(widths[:k]) for k in range(len(widths) + 1)]
        stage_v1, stage_l1, stage_v2 = (
            flat[:, starts[k]:starts[k + 1]].rearrange("p (a m) -> p a m", a=3) for k in range(3))
        stage_sw = flat[:, starts[3]:starts[4]]
        STAGED = [(stage_v1, [w_v1[:, :, p_, :] for p_ in (HI, LO)]), (stage_l1, [w_l1[:, :, p_, :] for p_ in (HI, LO)]),
                  (stage_v2, [w_v2[:, :, p_, :] for p_ in (HI, LO)]),
                  (stage_sw, [w_sw[:, p_, :] for p_ in (HI, LO)])]
        N_TAPS = 3 * len(vertical_taps()) + B4

        small = [(avg_sb[:], avg), (idn[:], ident), (sel[:].rearrange("p q n m -> p (q n m)"), select),
                 (w_pool[:], vpool), (gb1_sb[:], gb1), (gw2_sb[:], gw2t), (gb2_sb[:], gb2), (sb_sb[:], sb_),
                 (biases[:, 0:1], kb1), (biases[:, 1:2], kb2), (biases[:, 2:3], l1b)]
        small += [(gw1_sb[C * b:C * b + C, :], gw1t) for b in range(B4)]

        block = ctx.enter_context(nc.Block())

        def unit(n, u):
            return n * NU + u

        def tile(n, u, t):
            return n * NT + u * TU + t

        def wins_count(n, layer, i):
            per_image = NI * 16 * (FULL_COPIES + CONV_COPIES)
            return 16 + n * per_image + (layer * NI * FULL_COPIES + i * (CONV_COPIES if layer else FULL_COPIES)) * 16

        def steps(eng, body, first, last):
            if last - first == 1:
                body(first)
            elif last > first:
                with eng.Fori(first, last) as i:
                    body(i)

        def all_steps(eng, body):
            steps(eng, lambda i: body(i, False, False), 0, NI - LEAD // 2)
            for i in range(NI - LEAD // 2, NI):
                body(i, True, i == NI - 1)

        def images(eng, body):
            if NS > 2:
                with eng.Fori(0, NS - 1) as n:
                    body(n, False)
            elif NS == 2:
                body(0, False)
            body(NS - 1, True)

        def held(eng, count):
            if not isinstance(count, int):
                eng.compute_val(count)
            return count

        def q_tile(u, t):
            return bass.ds(u * QU + t * QT, QT)

        class Order:

            def __init__(self, eng, s, calls, per):
                self.eng, self.s, self.start, self.per, self.k = eng, s, calls * per, per, 0

            def mark(self, ins):
                self.k += 1
                return ins.then_inc(self.s, 1)

            def wait(self):
                self.eng.wait_ge(self.s, self.start + self.k)

            def close(self):
                assert self.k == self.per, (self.k, self.per)

        def weave(pattern, **streams):
            for name in pattern:
                next(streams[name])
            assert all(next(stream, None) is None for stream in streams.values())

        @block.sync
        def _(sp):
            def load_x(n, i):
                q = bass.ds(i * 2 * QU, 2 * QU)
                sp.dma_start(image[:, q, :], x[n, :, q, :] if isinstance(n, int) else
                             x[bass.ds(n, 1), :, q, :].rearrange("a p q w -> (a p) q w")).then_inc(x_in, 16)

            for j in range(2):
                sp.sem_inc(wins_in[j], 16)
            for dst, src in small:
                sp.dma_start(dst, src).then_inc(consts_in, 16)
            sp.wait_ge(stage_zero, 1)
            for k, b, kh in vertical_taps():
                rows, cols = slice(C * k, C * k + C), slice(C * b, C * b + C)
                sp.dma_start(stage_v1[rows, :, cols], k1t[:, kh, :, :]).then_inc(taps_in, 16)
                sp.dma_start(stage_l1[rows, :, cols], l1t[:, kh, :, :]).then_inc(taps_in, 16)
                sp.dma_start(stage_v2[rows, :, cols], k2t[:, kh, :, :]).then_inc(taps_in, 16)
            for b in range(B4):
                sp.dma_start(stage_sw[C * b:C * b + C, N_OPS * b:N_OPS * b + N_OPS], swt).then_inc(taps_in, 16)
            for i in range(NI):
                if i:
                    sp.wait_ge(x_in, 16 * i)
                load_x(0, i)
            sp.wait_ge(set_up, 1)

            def window_copies(n, layer, i, j, end):
                u = 2 * i + j
                split = held(sp, n * 2 * NT + layer * NT + (NT if end else (u + 2) * TU))
                lo_split = held(sp, n * 2 * NT + layer * NT + (NT if end else (u + 2) * TU) + 1)
                dil_done = held(sp, 3 + (n + 1) * NT if layer else 1 + tile(n, u, 0))
                l1_done = held(sp, 1 + tile(n, u, 0) if layer else 3 + n * NT)
                sp.wait_ge(dil_psum, dil_done)
                sp.wait_ge(l1_psum, l1_done)
                sp.wait_ge(hi_ready, split)
                sp.wait_ge(lo_ready, lo_split)
                before, here, after = (bass.ds(u * QU + d, QU) for d in range(3))

                def copy(kind, dst, src, q):
                    sp.dma_start(wins[j][dst, kind, :, :, :], norm[src, q, :, :]).then_inc(wins_in[j], 16)

                copy(UPPER, slice(0, C), slice(3 * C, P), before)
                copy(UPPER, slice(C, P), slice(0, 3 * C), here)
                copy(LOWER, slice(0, 3 * C), slice(C, P), here)
                copy(LOWER, slice(3 * C, P), slice(0, C), after)
                if layer == 0:
                    for r, kind in enumerate((EVEN, ODD)):
                        low, high = slice(C * r, C * r + C), slice(C * (2 + r), C * (2 + r) + C)
                        copy(kind, slice(0, C), high, before)
                        copy(kind, slice(C, 2 * C), low, here)
                        copy(kind, slice(2 * C, 3 * C), high, here)
                        copy(kind, slice(3 * C, P), low, after)

            def image_body(n, last):
                def step0(i, end=False):
                    window_copies(n, 0, i, 0, False)
                    window_copies(n, 0, i, 1, end)

                steps(sp, step0, 0, NI - 1)
                step0(NI - 1, True)

                def step1(i, first=False, end=False):
                    window_copies(n, 1, i, 0, False)
                    window_copies(n, 1, i, 1, end)
                    if not first and not last:
                        next_x(i - 1)

                def next_x(i):
                    outputs_made = held(sp, 2 + tile(n, 2 * i + 2, 0))
                    loaded = held(sp, (n * NI + i + NI) * 16)
                    sp.wait_ge(out_ready, outputs_made)
                    sp.wait_ge(x_in, loaded)
                    load_x(n + 1, i)

                step1(0, first=True)
                steps(sp, step1, 1, NI - 1)
                step1(NI - 1, end=True)
                if not last:
                    next_x(NI - 1)

            images(sp, image_body)

        @block.vector
        def _(dve):
            for s_, k in ((conv_free, 2), (comb_done, 2), (lo_ready, 1)):
                dve.sem_inc(s_, k)
            nc.vector.memset(flat[:, 0:starts[-1]], 0.0).then_inc(stage_zero, 1)
            init = Order(dve, init_step, 0, 21)
            init.mark(nc.vector.memset(norm[:, 0, :, :], 0.0))
            init.mark(nc.vector.memset(norm[:, NQ + 1, :, :], 0.0))
            init.mark(nc.vector.memset(norm[:, 1:NQ + 1, :, 0:PADW], 0.0))
            init.mark(nc.vector.memset(norm[:, 1:NQ + 1, :, PADW + W:WP], 0.0))
            init.mark(nc.vector.memset(vsum[:, :, 0:1], 0.0))
            init.mark(nc.vector.memset(vsum[:, :, W + 1:W + 2], 0.0))
            init.mark(nc.vector.memset(beats1[:], 0.0))
            init.mark(nc.vector.memset(beats2[:], 0.0))
            for m, v in enumerate((2.0, 0.0, 0.0, 0.0, -1.0, 0.0, 1.0)):
                init.mark(nc.vector.memset(beats3[:, m, :], v))
            dve.wait_ge(taps_in, 16 * N_TAPS)
            dve.wait_ge(consts_in, 16 * len(small))
            for src, _ in STAGED:
                init.mark(nc.vector.tensor_scalar(src, src, W_SCALE, None, ALU.mult))
            init.wait()
            for src, dst in STAGED:
                nc.vector.tensor_copy(dst[HI], src).then_inc(split_w, 1)
            dve.wait_ge(split_w, len(STAGED))
            for src, dst in STAGED:
                nc.vector.tensor_tensor(dst[LO], src, dst[HI], ALU.subtract).then_inc(split_w, 1)
            init.mark(nc.vector.tensor_scalar(kbs[:], biases[:, 0:2], X_SCALE * W_SCALE, None, ALU.mult))
            init.mark(nc.vector.tensor_tensor(sb_sb[:], sb_sb[:], gb2_sb[:], ALU.add))
            dve.wait_ge(split_w, 2 * len(STAGED))
            init.wait()
            nc.vector.memset(rden[:], 0.0).then_inc(set_up, 1)
            init.close()

            def tile_stats(u, t):
                nc.vector.bn_stats(bst[:, bass.ds(u * TU + t, 1), :].rearrange("p a s -> p (a s)"),
                                   image[:, q_tile(u, t), :].rearrange("p q w -> p (q w)")).then_inc(bst_step, 1)

            def x_stats(n, i):
                dve.wait_ge(x_in, (n * NI + i + 1) * 16)
                for j in range(2):
                    for t in range(TU):
                        tile_stats(2 * i + j, t)

            def finish_stats(n, layer):
                s = Order(dve, stats_step, n * 2 + layer, 8)
                dve.wait_ge(bst_step, n * 2 * NT + layer * NT + NT)
                c = coef[layer]
                nc.vector.memset(T1, 0.0)
                nc.vector.bn_aggr(mv[:], bst[:].rearrange("p a s -> p (a s)")).then_inc(mean_in, 1)
                dve.wait_ge(mean_in, n * 2 + layer + 1)
                dve.wait_ge(stat_sum, n * 6 + layer * 4 + 1)
                s.mark(nc.vector.tensor_copy(MG, p_stat[:, 0:1]))
                s.wait()
                s.mark(nc.vector.tensor_tensor(D_, mv[:, 0:1], MG, ALU.subtract))
                s.wait()
                nc.vector.scalar_tensor_tensor(V2, D_, D_, mv[:, 1:2], ALU.mult, ALU.add).then_inc(sq_in, 1)
                dve.wait_ge(stat_sum, n * 6 + layer * 4 + 2)
                nc.vector.tensor_scalar(VE, p_stat[:, 1:2], GN_EPS, None, ALU.add).then_inc(sq_in, 1)
                dve.wait_ge(sq_done, n * 2 + layer + 1)
                s.mark(nc.vector.reciprocal(R_, SD))
                s.wait()
                s.mark(nc.vector.scalar_tensor_tensor(T1, R_, R_, VE, ALU.mult, ALU.mult))
                s.wait()
                s.mark(nc.vector.tensor_scalar(T2, T1, -0.5, 1.5, ALU.mult, ALU.add))
                s.wait()
                s.mark(nc.vector.tensor_tensor(c[:, 0:1], R_, T2, ALU.mult))
                s.wait()
                s.mark(nc.vector.scalar_tensor_tensor(c[:, 1:2], MG, -1.0, c[:, 0:1], ALU.mult, ALU.mult))
                s.mark(nc.vector.tensor_tensor(GN_, D_, c[:, 0:1], ALU.mult))
                s.wait()
                nc.vector.tensor_scalar(c[:, 2:4], c[:, 0:2], X_SCALE, None, ALU.mult).then_inc(coef_ready, 1)
                s.close()

            def gate(n):
                dve.wait_ge(hid_done, n + 1)
                nc.vector.tensor_copy(hid_rep[:], hid[:].to_broadcast([HID, P])).then_inc(sq_in, 1)
                dve.wait_ge(stat_sum, n * 6 + 4)
                nc.vector.tensor_tensor(rbias[:], p_stat[:, 4:8], sb_sb[:], ALU.add).then_inc(gate_ready, 1)

            def split_stages(n, layer, u):
                c = coef[layer]
                for t in range(TU):
                    k = n * 2 * NT + layer * NT + u * TU + t
                    src = image[:, q_tile(u, t), :]
                    dst = norm[:, bass.ds(u * QU + t * QT + 1, QT), :, PADW:PADW + W]
                    dve.wait_ge(lo_ready, 1 + k)
                    nc.vector.tensor_scalar(scaled[:], src, c[:, 2:3], c[:, 3:4], ALU.mult,
                                            ALU.add).then_inc(split_step, 1)
                    yield True
                    dve.wait_ge(split_step, k + 1)
                    dve.wait_ge(hi_ready, k + 1)
                    nc.vector.tensor_tensor(dst[:, :, LO, :], scaled[:], dst[:, :, HI, :],
                                            ALU.subtract).then_inc(lo_ready, 1)
                    yield True

            def split_unit(n, layer, u):
                weave("ssss", s=split_stages(n, layer, u))

            def router_stages(n, u):
                k = unit(n, u)
                s = Order(dve, router_step, k, 17)
                dve.wait_ge(logits_ready, k + 1)
                bias = rbias[:].rearrange("p (n o) -> p n o", o=1).to_broadcast([P, N_OPS, XCOLS])
                s.mark(nc.vector.scalar_tensor_tensor(logit[:], p_logit.rearrange("p x n -> p n x"),
                                                      1.0 / (X_SCALE * W_SCALE), bias, ALU.mult, ALU.add))
                yield True
                s.wait()
                for d, g in ((1, beats1), (2, beats2), (3, beats3)):
                    s.mark(nc.vector.tensor_tensor(g[:, d:N_OPS, :], logit[:, 0:N_OPS - d, :],
                                                   logit[:, d:N_OPS, :], ALU.is_ge))
                s.mark(nc.vector.tensor_tensor(top[:], logit[:, 0:2, :], logit[:, 2:4, :], ALU.max))
                yield True
                s.wait()
                s.mark(nc.vector.tensor_tensor(diff1[:], beats1[:, 1:N_OPS + 1, :], beats1[:, 0:N_OPS, :],
                                               ALU.subtract))
                s.mark(nc.vector.tensor_tensor(diff2[:], beats2[:, 2:N_OPS + 2, :], beats2[:, 0:N_OPS, :],
                                               ALU.subtract))
                s.mark(nc.vector.tensor_tensor(top[:, 0, :], top[:, 0, :], top[:, 1, :], ALU.max))
                yield True
                s.wait()
                s.mark(nc.vector.tensor_tensor(diff1[:], diff1[:], diff2[:], ALU.add))
                peak = top[:, 0:1, :].to_broadcast([P, N_OPS, XCOLS])
                nc.vector.tensor_tensor(logit[:], logit[:], peak, ALU.subtract).then_inc(exp_in, 1)
                yield True
                s.wait()
                s.mark(nc.vector.tensor_tensor(diff2[:], beats3[:, 3:N_OPS + 3, :], beats3[:, 0:N_OPS, :],
                                               ALU.subtract))
                yield True
                s.wait()
                s.mark(nc.vector.tensor_tensor(diff1[:], diff1[:], diff2[:], ALU.add))
                yield True
                s.wait()
                dve.wait_ge(exp_done, k + 1)
                s.mark(nc.vector.scalar_tensor_tensor(expo[:], diff1[:], 0.0, expo[:], ALU.is_ge, ALU.mult))
                yield True
                s.wait()
                s.mark(nc.vector.tensor_tensor(top[:], expo[:, 0:2, :], expo[:, 2:4, :], ALU.add))
                yield True
                s.wait()
                s.mark(nc.vector.tensor_tensor(top[:, 0, :], top[:, 0, :], top[:, 1, :], ALU.add))
                yield True
                s.wait()
                s.mark(nc.vector.reciprocal(rden[:], top[:, 0, :]))
                yield True
                s.wait()
                recip = rden[:].rearrange("p (o x) -> p o x", o=1).to_broadcast([P, N_OPS, XCOLS])
                s.mark(nc.vector.scalar_tensor_tensor(logit[:], expo[:], PROB_SCALE, recip, ALU.mult, ALU.mult))
                yield True
                s.wait()
                lg = logit[:].rearrange("p n (q b) -> p n q b", q=QU)
                px = w_px[:].rearrange("p a q n b -> p a n q b")
                s.mark(nc.vector.tensor_copy(px[:, HI], lg))
                yield True
                s.wait()
                nc.vector.tensor_tensor(px[:, LO], lg, px[:, HI], ALU.subtract).then_inc(probs_ready, 1)
                s.close()
                yield True

            def combine_stages(n, u, t):
                k = tile(n, u, t)
                s = Order(dve, comb_step, k, 3)
                dst = image[:, q_tile(u, t), :]
                dve.wait_ge(v1_psum, k + 1)
                dve.wait_ge(router_w_ready, 2 + 4 * k + 2)
                dve.wait_ge(comb_done, 2 + k)
                s.mark(nc.vector.scalar_tensor_tensor(prod[:], p_v1[t][:], kbs[:, 0:1], router_w[1][:],
                                                      ALU.add, ALU.mult))
                yield True
                dve.wait_ge(dil_psum, 3 + k + 1)
                dve.wait_ge(router_w_ready, 2 + 4 * k + 3)
                nc.vector.scalar_tensor_tensor(router_w[2][:], p_dil[t][:], kbs[:, 1:2], router_w[2][:],
                                               ALU.add, ALU.mult).then_inc(conv_free, 1)
                yield True
                dve.wait_ge(conv_free, 2 + k + 1)
                s.wait()
                s.mark(nc.vector.tensor_tensor(prod[:], prod[:], router_w[2][:], ALU.add))
                yield True
                dve.wait_ge(pool_ready, 1 + k + 1)
                s.wait()
                s.mark(nc.vector.tensor_tensor(prod[:], prod[:], pool_p[t][:], ALU.add))
                yield True
                dve.wait_ge(base_ready, k + 1)
                s.wait()
                nc.vector.tensor_tensor(dst, prod[:], base[t][:], ALU.add).then_inc(comb_done, 1)
                yield True
                dve.wait_ge(comb_done, 2 + k + 1)
                tile_stats(u, t)
                s.close()
                yield True

            def image_body(n, last):
                finish_stats(n, 0)
                dve.wait_ge(coef_ready, 2 * n + 1)
                dve.wait_ge(wins_in[0], wins_count(n, 0, 0))
                dve.wait_ge(wins_in[1], wins_count(n, 0, 0))
                split_unit(n, 0, 0)
                split_unit(n, 0, 1)
                gate(n)
                dve.wait_ge(gate_ready, n + 1)
                split_unit(n, 0, 2)
                weave("rrrrsrrsrrrrsrrrs", r=router_stages(n, 0), s=split_stages(n, 0, 3))

                def step0(i, all_split, end):
                    for j in range(2):
                        u = 2 * i + j
                        if end and j == 1:
                            weave("cccccc", c=combine_stages(n, u, 0))
                        else:
                            weave("rrrcrcrrcrcrrcrcrrr", r=router_stages(n, u + 1), c=combine_stages(n, u, 0))
                        if all_split:
                            weave("cccccc", c=combine_stages(n, u, 1))
                        else:
                            weave("csccscscsc", c=combine_stages(n, u, 1), s=split_stages(n, 0, u + LEAD))

                all_steps(dve, step0)

                finish_stats(n, 1)
                dve.wait_ge(coef_ready, 2 * n + 2)
                dve.wait_ge(wins_in[0], wins_count(n, 1, 0))
                dve.wait_ge(wins_in[1], wins_count(n, 1, 0))
                split_unit(n, 1, 0)
                split_unit(n, 1, 1)
                steps(dve, lambda i: [split_unit(n, 1, 2 * i), split_unit(n, 1, 2 * i + 1)], 1, NI)
                if not last:
                    steps(dve, lambda i: x_stats(n + 1, i), 0, NI)

            steps(dve, lambda i: x_stats(0, i), 0, NI)
            images(dve, image_body)

        @block.scalar
        def _(act):
            for s_, k in ((router_w_ready, 2), (l1_evac, 2), (vsum_ready, 1), (out_st[0], 16), (out_st[1], 16)):
                act.sem_inc(s_, k)
            act.wait_ge(set_up, 1)

            def stats_root(n, layer):
                act.wait_ge(sq_in, n * 5 + layer * 3 + 2)
                nc.scalar.activation(SD, VE, ACT.Sqrt).then_inc(sq_done, 1)

            def hi_unit(n, layer, u):
                c = coef[layer]
                for t in range(TU):
                    nc.scalar.activation(norm[:, bass.ds(u * QU + t * QT + 1, QT), HI, PADW:PADW + W],
                                         image[:, q_tile(u, t), :], ACT.Identity, bias=c[:, 3:4],
                                         scale=c[:, 2:3]).then_inc(hi_ready, 1)

            def exps(n, u):
                act.wait_ge(exp_in, unit(n, u) + 1)
                nc.scalar.activation(expo[:], logit[:], ACT.Exp).then_inc(exp_done, 1)

            def weights_row(n, u):
                act.wait_ge(tr_ready, unit(n, u) + 1)
                nc.scalar.copy(w_row[:], p_tr).then_inc(w_row_ready, 1)

            UNSCALE = [1.0 / PROB_SCALE, 1.0 / (PROB_SCALE * X_SCALE * W_SCALE),
                       1.0 / (PROB_SCALE * X_SCALE * W_SCALE), 1.0 / (PROB_SCALE * X_SCALE * 9.0)]

            def evacuate(n, u, t):
                k = tile(n, u, t)
                act.wait_ge(w0_used, 1 + k)
                nc.scalar.activation(xn[t][:], image[:, q_tile(u, t), :], ACT.Identity, bias=coef[0][:, 1:2],
                                     scale=coef[0][:, 0:1]).then_inc(xn_ready, 1)
                act.wait_ge(pool_psum, k + 1)
                act.wait_ge(hsum_step, 2 * k + 2)
                nc.scalar.copy(vsum[:, :, 1:1 + W], p_pool[:]).then_inc(vsum_ready, 1)
                for m in range(N_OPS):
                    act.wait_ge(pw_ready, 4 * k + m + 1)
                    if m == 0:
                        act.wait_ge(w0_used, 2 + k)
                    elif m == 3:
                        act.wait_ge(pool_ready, k + 1)
                    elif m == 1:
                        act.wait_ge(conv_free, k + 2)
                    elif m == 2:
                        act.wait_ge(comb_done, k + 2)
                    nc.scalar.activation(router_w[m][:], p_w[m % 2][:], ACT.Copy,
                                         scale=UNSCALE[m]).then_inc(router_w_ready, 1)

            def conv_out(n, u, t):
                k = tile(n, u, t)
                act.wait_ge(l1_psum, 3 + k + 1)
                act.wait_ge(out_ready, k + 1)
                nc.scalar.activation(xn[t][:], p_v1[t][:], ACT.Identity, bias=biases[:, 2:3],
                                     scale=1.0 / (X_SCALE * W_SCALE)).then_inc(l1_evac, 1)

            def store(n, u, t):
                act.wait_ge(out_ready, 2 + tile(n, u, t) + 1)
                q = q_tile(u, t)
                act.dma_start(out[n, :, q, :] if isinstance(n, int) else
                              out[bass.ds(n, 1), :, q, :].rearrange("a p q w -> (a p) q w"),
                              router_w[t][:]).then_inc(out_st[t], 16)

            def image_body(n, last):
                stats_root(n, 0)
                act.wait_ge(stat_sum, n * 6 + 3)
                nc.scalar.activation(hid[:], p_stat[0:HID, 2:3], ACT.Relu, bias=gb1_sb[:],
                                     scale=1.0 / B4).then_inc(hid_done, 1)
                act.wait_ge(coef_ready, 2 * n + 1)
                act.wait_ge(wins_in[0], wins_count(n, 0, 0))
                act.wait_ge(wins_in[1], wins_count(n, 0, 0))
                act.wait_ge(out_st[0], 16 + unit(n, 0) * 16)
                act.wait_ge(out_st[1], 16 + unit(n, 0) * 16)
                hi_unit(n, 0, 0)
                hi_unit(n, 0, 1)
                hi_unit(n, 0, 2)
                hi_unit(n, 0, 3)
                exps(n, 0)
                weights_row(n, 0)

                def step0(i, all_split, end):
                    for j in range(2):
                        u = 2 * i + j
                        if not all_split:
                            hi_unit(n, 0, u + LEAD)
                        evacuate(n, u, 0)
                        if not (end and j == 1):
                            exps(n, u + 1)
                        evacuate(n, u, 1)
                        if not (end and j == 1):
                            weights_row(n, u + 1)

                all_steps(act, step0)

                stats_root(n, 1)
                act.wait_ge(coef_ready, 2 * n + 2)
                act.wait_ge(wins_in[0], wins_count(n, 1, 0))
                act.wait_ge(wins_in[1], wins_count(n, 1, 0))
                for u in range(LEAD):
                    hi_unit(n, 1, u)

                def step1(i, all_split, end):
                    for j in range(2):
                        u = 2 * i + j
                        if not all_split:
                            hi_unit(n, 1, u + LEAD)
                        conv_out(n, u, 0)
                        conv_out(n, u, 1)
                        store(n, u, 0)
                        store(n, u, 1)

                all_steps(act, step1)

            images(act, image_body)
            act.wait_ge(out_st[0], 16 + NS * NU * 16)
            act.wait_ge(out_st[1], 16 + NS * NU * 16)

        @block.gpsimd
        def _(pool):
            for s_, k in ((hsum_step, 2), (w0_used, 2), (pool_ready, 1), (out_ready, 2)):
                pool.sem_inc(s_, k)
            pool.wait_ge(set_up, 1)

            def base_and_pool(n, u, t):
                k = tile(n, u, t)
                pool.wait_ge(xn_ready, k + 1)
                pool.wait_ge(comb_done, k + 1)
                pool.wait_ge(vsum_ready, 1 + k + 1)
                nc.gpsimd.tensor_tensor(pool_p[t][:], vsum[:, :, 0:W], vsum[:, :, 1:1 + W], ALU.add).then_inc(hsum_step, 1)
                pool.wait_ge(hsum_step, 2 + 2 * k + 1)
                nc.gpsimd.tensor_tensor(pool_p[t][:], pool_p[t][:], vsum[:, :, 2:2 + W], ALU.add).then_inc(hsum_step, 1)
                pool.wait_ge(router_w_ready, 2 + 4 * k + 1)
                nc.gpsimd.tensor_tensor(base[t][:], xn[t][:], router_w[0][:], ALU.mult).then_inc(w0_used, 1)
                pool.wait_ge(w0_used, 2 + k + 1)
                nc.gpsimd.tensor_tensor(base[t][:], base[t][:], image[:, q_tile(u, t), :],
                                        ALU.add).then_inc(base_ready, 1)
                pool.wait_ge(router_w_ready, 2 + 4 * k + 4)
                pool.wait_ge(hsum_step, 2 + 2 * k + 2)
                nc.gpsimd.tensor_tensor(pool_p[t][:], pool_p[t][:], router_w[3][:], ALU.mult).then_inc(pool_ready, 1)

            def residual(n, u, t):
                k = tile(n, u, t)
                pool.wait_ge(l1_evac, 2 + k + 1)
                pool.wait_ge(out_st[t], 16 + unit(n, u) * 16)
                nc.gpsimd.tensor_tensor(router_w[t][:], xn[t][:], image[:, q_tile(u, t), :],
                                        ALU.add).then_inc(out_ready, 1)

            def image_body(n, last):
                def step0(i):
                    for j in range(2):
                        for t in range(TU):
                            base_and_pool(n, 2 * i + j, t)

                def step1(i):
                    for j in range(2):
                        for t in range(TU):
                            residual(n, 2 * i + j, t)

                steps(pool, step0, 0, NI)
                steps(pool, step1, 0, NI)

            images(pool, image_body)

        @block.tensor
        def _(pe):
            for s_ in (dil_psum, l1_psum):
                pe.sem_inc(s_, 3)
            pe.wait_ge(set_up, 1)
            mm = nc.tensor.matmul

            def moving(j, kind, t, part_, kw, dil):
                off = PADW + (kw - 1) * dil
                return wins[j][:, kind, t * QT:(t + 1) * QT, part_, off:off + W]

            def group_stats(n, layer):
                pe.wait_ge(mean_in, 2 * n + layer + 1)
                mm(p_stat[:, 0:1], avg_sb[:], mv[:, 0:1], start=True, stop=True).then_inc(stat_sum, 1)
                pe.wait_ge(sq_in, n * 5 + layer * 3 + 1)
                mm(p_stat[:, 1:2], avg_sb[:], V2, start=True, stop=True).then_inc(stat_sum, 1)

            def gate(n):
                pe.wait_ge(coef_ready, 2 * n + 1)
                mm(p_stat[0:HID, 2:3], gw1_sb[:], GN_, start=True, stop=True).then_inc(stat_sum, 1)
                pe.wait_ge(sq_in, n * 5 + 3)
                mm(p_stat[:, 4:8], hid_rep[:], gw2_sb[:], start=True, stop=True).then_inc(stat_sum, 1)

            def logits(n, u):
                both_parts = n * 2 * NT + (u + 1) * TU
                pe.wait_ge(hi_ready, both_parts)
                pe.wait_ge(lo_ready, both_parts + 1)
                for q in range(QU):
                    for h in range(HALVES):
                        for m, (xp, wp) in enumerate(PRODUCTS):
                            px = norm[:, bass.ds(u * QU + q + 1, 1), xp, PADW + h * P:PADW + h * P + P]
                            px = px.rearrange("p a w -> p (a w)")
                            last = mm(p_logit_qh[:, q, h], px, w_sw[:, wp, :],
                                      start=m == 0, stop=m == len(PRODUCTS) - 1)
                last.then_inc(logits_ready, 1)

            def transpose_weights(n, u):
                pe.wait_ge(probs_ready, unit(n, u) + 1)
                for h in range(HALVES):
                    src = w_px[:].rearrange("p a q n (b h) -> p h (a q n b)", h=HALVES)[:, h]
                    last = nc.tensor.transpose(p_tr[:, h * P:(h + 1) * P], src, idn[:])
                last.then_inc(tr_ready, 1)

            def vertical(dst, weights, j, t, parts):
                todo = [(kw, xp, wp) for kw in range(3) for xp, wp in parts]
                for m, (kw, xp, wp) in enumerate(todo):
                    for half, kind in enumerate((UPPER, LOWER)):
                        last = mm(dst[half * 2 * C:(half + 1) * 2 * C, :, :], weights[:, kw, wp, :],
                                  moving(j, kind, t, xp, kw, 1), start=m == 0, stop=m == len(todo) - 1)
                return last

            def vertical2(dst, j, t):
                todo = [(kw, xp, wp) for kw in range(3) for xp, wp in PRODUCTS]
                for m, (kw, xp, wp) in enumerate(todo):
                    for b in range(B4):
                        last = mm(dst[b * C:b * C + C, :, :], w_v2[:, kw, wp, C * (b // 2):C * (b // 2) + C],
                                  moving(j, (EVEN, ODD)[b % 2], t, xp, kw, 2), start=m == 0, stop=m == len(todo) - 1)
                    yield last

            def op_weight(n, u, t, m):
                k = tile(n, u, t)
                pe.wait_ge(router_w_ready, 4 * k + m + 1)
                for g in range(QT):
                    last = mm(p_w[m % 2][:, g, :], sel[:, t * QT + g, m, :], w_row[:], start=True, stop=True)
                last.then_inc(pw_ready, 1)

            def layer0_tile(n, u, j, t, route_next):
                k = tile(n, u, t)
                pe.wait_ge(vsum_ready, 1 + k)
                for m, xp in enumerate((HI, LO)):
                    for half, kind in enumerate((UPPER, LOWER)):
                        last = mm(p_pool[half * 2 * C:(half + 1) * 2 * C, :, :], w_pool[:],
                                  moving(j, kind, t, xp, 1, 1), start=m == 0, stop=m == 1)
                last.then_inc(pool_psum, 1)
                pe.wait_ge(conv_free, k + 1)
                vertical(p_v1[t], w_v1, j, t, PRODUCTS).then_inc(v1_psum, 1)
                pe.wait_ge(w_row_ready, unit(n, u) + 1)
                op_weight(n, u, t, 0)
                op_weight(n, u, t, 1)
                if route_next:
                    logits(n, u + 1)
                for m, last in enumerate(vertical2(p_dil[t], j, t)):
                    if m == 3:
                        op_weight(n, u, t, 2)
                        op_weight(n, u, t, 3)
                last.then_inc(dil_psum, 1)

            def windows_in(n, layer, i, j):
                pe.wait_ge(wins_in[j], wins_count(n, layer, i + 1))

            def image_body(n, last_image):
                group_stats(n, 0)
                gate(n)
                pe.wait_ge(gate_ready, n + 1)
                logits(n, 0)
                transpose_weights(n, 0)

                def step0(i, end=False):
                    for j in range(2):
                        u = 2 * i + j
                        more = not (end and j == 1)
                        windows_in(n, 0, i, j)
                        layer0_tile(n, u, j, 0, more)
                        layer0_tile(n, u, j, 1, False)
                        if more:
                            transpose_weights(n, u + 1)

                steps(pe, step0, 0, NI - 1)
                step0(NI - 1, True)

                group_stats(n, 1)

                def step1(i):
                    for j in range(2):
                        u = 2 * i + j
                        windows_in(n, 1, i, j)
                        for t in range(TU):
                            k = tile(n, u, t)
                            pe.wait_ge(l1_evac, k + 1)
                            vertical(p_v1[t], w_l1, j, t, PRODUCTS).then_inc(l1_psum, 1)

                steps(pe, step1, 0, NI)

            images(pe, image_body)


def layout(inputs):
    x = np.asarray(inputs["x"])
    n, c, h, w = x.shape
    q = h // B4
    g = {k: np.asarray(v) for k, v in inputs.items()}
    taps = lambda a: np.ascontiguousarray(a.transpose(1, 2, 3, 0))
    per_partition = lambda a: np.ascontiguousarray(np.tile(a, B4)[:, None])
    everywhere = lambda a: np.ascontiguousarray(np.tile(a[None, :], (P, 1)))
    avg = np.zeros((P, P), np.float32)
    group = (np.arange(P) % C) // 2
    avg[group[:, None] == group[None, :]] = 1.0 / (2 * B4)
    ident = np.eye(P, dtype=np.float16)
    select = np.zeros((P, QU, N_OPS, P), np.float16)
    for part_ in range(2):
        for qq in range(QU):
            for op in range(N_OPS):
                for b in range(B4):
                    select[((part_ * QU + qq) * N_OPS + op) * B4 + b, qq, op, C * b:C * b + C] = 1
    vpool = np.zeros((P, 2 * C), np.float16)
    for k, b, _ in vertical_taps():
        vpool[C * k + np.arange(C), C * b + np.arange(C)] = 1
    return {
        "x": np.ascontiguousarray(x.reshape(n, c, q, B4, w).transpose(0, 3, 1, 2, 4)).reshape(n, P, q, w),
        "gw1t": np.ascontiguousarray(g["L0_conv_gw1"].T), "gb1": np.ascontiguousarray(g["L0_conv_gb1"][:, None]),
        "gw2t": np.ascontiguousarray(g["L0_conv_gw2"].T), "gb2": everywhere(g["L0_conv_gb2"]),
        "sb_": everywhere(g["L0_conv_sb"]), "swt": np.ascontiguousarray(g["L0_conv_sw"].T),
        "k1t": taps(g["L0_conv_k1"]), "kb1": per_partition(g["L0_conv_kb1"]),
        "k2t": taps(g["L0_conv_k2"]), "kb2": per_partition(g["L0_conv_kb2"]),
        "l1t": taps(g["L1_conv_weight"]), "l1b": per_partition(g["L1_conv_bias"]),
        "avg": avg, "ident": ident, "select": select.reshape(P, -1), "vpool": vpool,
    }


def kernel(**inputs):
    import concourse.bacc as _bacc
    from concourse.bass_utils import run_bass_kernel_spmd as _run

    nc = _bacc.Bacc("TRN2", target_bir_lowering=False, num_devices=1)
    arrays = layout(inputs)
    args = {k: nc.dram_tensor(f"in_{k}", a.shape, mybir.dt.from_np(a.dtype), kind="ExternalInput").ap()
            for k, a in arrays.items()}
    n, p, q, w = arrays["x"].shape
    out = nc.dram_tensor("out_y", (n, p, q, w), F32, kind="ExternalOutput").ap()
    build(nc, out=out, **args)
    r = _run(nc, [{f"in_{k}": a for k, a in arrays.items()}], core_ids=[0])
    y = r.results[0]["out_y"]
    return y.reshape(n, B4, C, q, w).transpose(0, 2, 3, 1, 4).reshape(n, C, q * B4, w)
```

```python
from contextlib import ExitStack

import numpy as np

import concourse.bass as bass
from concourse import mybir

F32 = mybir.dt.float32
F16 = mybir.dt.float16
ALU = mybir.AluOpType
ACT = mybir.ActivationFunctionType

P = 128
C = 32
B4 = P // C
N_OPS = 4
QU = 4
QT = 2
TU = QU // QT
SLOTS = 4
LAG = 3
OUT_SLOTS = 2 * TU
FIRST_W, SECOND_W, LOGITS = (4, 0), (8, 5), 7
LEAD = 4
PADW = 2
UPPER, LOWER, EVEN, ODD = range(4)
HI, LO = 0, 1
X_SCALE = 16.0
W_SCALE = 32.0
PROB_SCALE = 1024.0
PRODUCTS = ((HI, HI), (LO, HI), (HI, LO))
GN_EPS = 1e-5


def vertical_taps():
    return [(k, b, k - b) for k in range(B4) for b in range(2) if 0 <= k - b <= 2]


def build(nc, x, gw1t, gb1, gw2t, gb2, sb_, swt, k1t, kb1, k2t, kb2, l1t, l1b, avg, ident, select, vpool, out):
    NS, _, NQ, W = x.shape
    NU = NQ // QU
    NI = NU // 2
    NT = NU * TU
    HID = gw1t.shape[1]
    WP = W + 2 * PADW
    HALVES = W // P
    K_OP = 2 * QU * B4
    XCOLS = HALVES * QU * B4
    CONV_COPIES, DIL_COPIES = 4, 8
    NR = NU // SLOTS

    with ExitStack() as ctx:
        def sb(name, shape, dt=F32):
            return ctx.enter_context(nc.sbuf_tensor(name, shape, dt))

        def pb(name, shape, dt=F32):
            return ctx.enter_context(nc.psum_tensor(name, shape, dt))

        def sem(name):
            return ctx.enter_context(nc.semaphore(name))

        image = sb("image", [P, NQ, W])
        norm = sb("norm", [P, NQ + 2, 2, WP], F16)
        wins = [sb(f"wins{j}", [P, 4, QU, 2, WP], F16) for j in range(2)]
        router_w = [sb(f"router_w{n}", [P, QT, W]) for n in range(N_OPS)]
        xn = [sb(f"xn{t}", [P, QT, W]) for t in range(2)]
        vsum = sb("vsum", [P, QT, W + 2])
        pool_p = [sb(f"pool_p{t}", [P, QT, W]) for t in range(2)]
        base = [sb(f"base{t}", [P, QT, W]) for t in range(2)]
        prod = sb("prod", [P, QT, W])
        scaled = [sb(f"scaled{t}", [P, QT, W]) for t in range(2)]
        w_v1 = sb("w_v1", [P, 3, 2, 2 * C], F16)
        w_l1 = sb("w_l1", [P, 3, 2, 2 * C], F16)
        w_v2 = sb("w_v2", [P, 3, 2, 2 * C], F16)
        w_sw = sb("w_sw", [P, 2, B4 * N_OPS], F16)
        w_pool = sb("w_pool", [P, 2 * C], F16)
        sel = sb("sel", [P, QU, P], F16)
        idn = sb("idn", [P, P], F16)
        avg_sb = sb("avg_sb", [P, P])
        gw1_sb = sb("gw1_sb", [P, HID])
        gb1_sb = sb("gb1_sb", [HID, 1])
        gw2_sb = sb("gw2_sb", [HID, N_OPS])
        gb2_sb = sb("gb2_sb", [P, N_OPS])
        sb_sb = sb("sb_sb", [P, N_OPS])
        biases = sb("biases", [P, 3])
        kbs = sb("kbs", [P, 2])
        bst = sb("bst", [P, NT, 6])
        mv = sb("mv", [P, 2])
        st = sb("st", [P, 16])
        D_, V2, VE, SD, R_, T1, T2, GN_, MG = (st[:, k:k + 1] for k in range(9))
        coef = [sb(f"coef{k}", [P, 4]) for k in range(2)]
        hid = sb("hid", [HID, 1])
        hid_rep = sb("hid_rep", [HID, P])
        rbias = sb("rbias", [P, N_OPS])
        logit = sb("logit", [P, N_OPS, XCOLS])
        beats1 = sb("beats1", [P, N_OPS + 1, XCOLS])
        beats2 = sb("beats2", [P, N_OPS + 2, XCOLS])
        beats3 = sb("beats3", [P, N_OPS + 3, XCOLS])
        diff1 = sb("diff1", [P, N_OPS, XCOLS])
        diff2 = sb("diff2", [P, N_OPS, XCOLS])
        top = sb("top", [P, 2, XCOLS])
        expo = sb("expo", [P, N_OPS, XCOLS])
        rden = sb("rden", [P, XCOLS])
        w_px = sb("w_px", [P, N_OPS, QU, 2, B4 * HALVES], F16)
        w_row = sb("w_row", [P, W], F16)

        p_v1 = [pb(f"p_v1_{t}", [P, QT, W]) for t in range(2)]
        p_dil = [pb(f"p_dil_{t}", [P, QT, W]) for t in range(2)]
        p_pool = pb("p_pool", [P, QT, W])
        p_w = [pb(f"p_w{j}", [P, QT, W]) for j in range(2)]
        p_misc = pb("p_misc", [P, 512])
        p_logit = p_misc[:, 0:XCOLS * N_OPS].rearrange("p (x n) -> p x n", n=N_OPS)
        p_logit_qh = p_misc[:, 0:XCOLS * N_OPS].rearrange("p (q b h n) -> p q h b n", q=QU, b=B4, n=N_OPS)
        p_stat = p_misc[:, 160:176]
        p_tr = p_misc[:, 256:256 + W // 2].bitcast(F16)

        consts_in = sem("consts_in")
        stage_zero = sem("stage_zero")
        taps_in = sem("taps_in")
        split_w = sem("split_w")
        gate_ready = sem("gate_ready")
        set_up = sem("set_up")
        init_step = sem("init_step")
        x_in = [sem(f"x_in{j}") for j in range(2)]
        wins_in = [sem(f"wins_in{j}") for j in range(2)]
        dil_wins_in = [sem(f"dil_wins_in{j}") for j in range(2)]
        l1_wins_in = [sem(f"l1_wins_in{s_}") for s_ in range(SLOTS)]
        out_st = [sem(f"out_st{s_}") for s_ in range(OUT_SLOTS)]
        stats_step = sem("stats_step")
        mean_in = sem("mean_in")
        stat_sum = sem("stat_sum")
        sq_in = sem("sq_in")
        sq_done = sem("sq_done")
        hid_done = sem("hid_done")
        coef_ready = sem("coef_ready")
        bst_step = sem("bst_step")
        scaled_ready = sem("scaled_ready")
        hi_ready = sem("hi_ready")
        lo_ready = sem("lo_ready")
        logits_ready = sem("logits_ready")
        router_step = sem("router_step")
        exp_in = sem("exp_in")
        exp_done = sem("exp_done")
        probs_ready = sem("probs_ready")
        tr_ready = sem("tr_ready")
        w_row_ready = sem("w_row_ready")
        pool_psum = sem("pool_psum")
        vsum_ready = sem("vsum_ready")
        hsum_step = sem("hsum_step")
        pw_ready = sem("pw_ready")
        router_w_ready = sem("router_w_ready")
        xn_ready = sem("xn_ready")
        w0_used = sem("w0_used")
        base_ready = sem("base_ready")
        pool_ready = sem("pool_ready")
        v1_psum = sem("v1_psum")
        dil_psum = sem("dil_psum")
        conv_free = sem("conv_free")
        comb_step = sem("comb_step")
        comb_done = sem("comb_done")
        l1_psum = sem("l1_psum")
        l1_evac = sem("l1_evac")
        out_ready = sem("out_ready")

        flat = wins[0][:].rearrange("p a q h w -> p (a q h w)").bitcast(F32)
        widths = (3 * 2 * C, 3 * 2 * C, 3 * 2 * C, B4 * N_OPS)
        starts = [sum(widths[:k]) for k in range(len(widths) + 1)]
        stage_v1, stage_l1, stage_v2 = (
            flat[:, starts[k]:starts[k + 1]].rearrange("p (a m) -> p a m", a=3) for k in range(3))
        stage_sw = flat[:, starts[3]:starts[4]]
        STAGED = [(stage_v1, [w_v1[:, :, p_, :] for p_ in (HI, LO)]), (stage_l1, [w_l1[:, :, p_, :] for p_ in (HI, LO)]),
                  (stage_v2, [w_v2[:, :, p_, :] for p_ in (HI, LO)]),
                  (stage_sw, [w_sw[:, p_, :] for p_ in (HI, LO)])]
        N_TAPS = 3 * len(vertical_taps()) + B4

        small = [(avg_sb[:], avg), (idn[:], ident), (sel[:].rearrange("p q m -> p (q m)"), select),
                 (w_pool[:], vpool), (gb1_sb[:], gb1), (gw2_sb[:], gw2t), (gb2_sb[:], gb2), (sb_sb[:], sb_),
                 (biases[:, 0:1], kb1), (biases[:, 1:2], kb2), (biases[:, 2:3], l1b)]
        small += [(gw1_sb[C * b:C * b + C, :], gw1t) for b in range(B4)]

        block = ctx.enter_context(nc.Block())

        def unit(n, u):
            return n * NU + u

        def tile(n, u, t):
            return n * NT + u * TU + t

        def wins_count(n, i):
            return 16 + (n * NI + i) * CONV_COPIES * 16

        def dil_wins_count(n, i):
            return 16 + (n * NI + i) * DIL_COPIES * 16

        def l1_wins_count(n, r):
            return 16 + (n * NR + r) * CONV_COPIES * 16

        def stored_count(n, i):
            return 16 + (n * NI + i) * 16

        def steps(eng, body, first, last):
            if last - first == 1:
                body(first)
            elif last > first:
                with eng.Fori(first, last) as i:
                    body(i)

        def all_steps(eng, body):
            steps(eng, lambda i: body(i, False, False), 0, NI - LEAD // 2)
            for i in range(NI - LEAD // 2, NI):
                body(i, True, i == NI - 1)

        def images(eng, body):
            if NS > 2:
                with eng.Fori(0, NS - 1) as n:
                    body(n, False)
            elif NS == 2:
                body(0, False)
            body(NS - 1, True)

        def held(eng, count):
            if not isinstance(count, int):
                eng.compute_val(count)
            return count

        def q_tile(u, t):
            return bass.ds(u * QU + t * QT, QT)

        class Order:

            def __init__(self, eng, s, calls, per):
                self.eng, self.s, self.start, self.per, self.k = eng, s, calls * per, per, 0

            def mark(self, ins):
                self.k += 1
                return ins.then_inc(self.s, 1)

            def wait(self):
                self.eng.wait_ge(self.s, self.start + self.k)

            def close(self):
                assert self.k == self.per, (self.k, self.per)

        def dve_scales(layer, u):
            return layer == 1 or isinstance(u, int) and u < LEAD // 2

        def l1_slot(slot):
            return wins[slot % 2][:, slot // 2 * 2:slot // 2 * 2 + 2, :, :, :]

        def weave(pattern, **streams):
            for name in pattern:
                next(streams[name])
            assert all(next(stream, None) is None for stream in streams.values())

        @block.sync
        def _(sp):
            def load_x(n, u, j):
                q = bass.ds(u * QU, QU)
                sp.dma_start(image[:, q, :], x[n, :, q, :] if isinstance(n, int) else
                             x[bass.ds(n, 1), :, q, :].rearrange("a p q w -> (a p) q w")).then_inc(x_in[j], 16)

            for s_ in wins_in + dil_wins_in + l1_wins_in:
                sp.sem_inc(s_, 16)
            def first_x(u):
                if u >= 2:
                    sp.wait_ge(x_in[u % 2], 16 * (u // 2))
                load_x(0, u, u % 2)

            for k, (dst, src) in enumerate(small):
                if k % 4 == 0:
                    first_x(k // 4)
                sp.dma_start(dst, src).then_inc(consts_in, 16)
            first_left = -(-len(small) // 4)
            sp.wait_ge(stage_zero, 1)
            for k, b, kh in vertical_taps():
                rows, cols = slice(C * k, C * k + C), slice(C * b, C * b + C)
                first_x(first_left)
                first_left += 1
                sp.dma_start(stage_v1[rows, :, cols], k1t[:, kh, :, :]).then_inc(taps_in, 16)
                sp.dma_start(stage_l1[rows, :, cols], l1t[:, kh, :, :]).then_inc(taps_in, 16)
                sp.dma_start(stage_v2[rows, :, cols], k2t[:, kh, :, :]).then_inc(taps_in, 16)
            for b in range(B4):
                sp.dma_start(stage_sw[C * b:C * b + C, N_OPS * b:N_OPS * b + N_OPS], swt).then_inc(taps_in, 16)
            for u in range(first_left, NU):
                first_x(u)
            sp.wait_ge(set_up, 1)

            def split_counts(n, layer, u, end):
                tiles = n * 2 * NT + layer * NT + (NT if end else (u + 1) * TU + 1)
                return held(sp, tiles), held(sp, tiles + 2)

            def copies(dst, kinds, signal, u):
                before, here, after = (bass.ds(u * QU + d, QU) for d in range(3))

                def copy(kind, rows, src, q):
                    sp.dma_start(dst[rows, kind, :, :, :], norm[src, q, :, :]).then_inc(signal, 16)

                for kind in kinds:
                    if kind == UPPER:
                        copy(kind, slice(0, C), slice(3 * C, P), before)
                        copy(kind, slice(C, P), slice(0, 3 * C), here)
                    elif kind == LOWER:
                        copy(kind, slice(0, 3 * C), slice(C, P), here)
                        copy(kind, slice(3 * C, P), slice(0, C), after)
                    else:
                        r = kind - EVEN
                        low, high = slice(C * r, C * r + C), slice(C * (2 + r), C * (2 + r) + C)
                        copy(kind, slice(0, C), high, before)
                        copy(kind, slice(C, 2 * C), low, here)
                        copy(kind, slice(2 * C, 3 * C), high, here)
                        copy(kind, slice(3 * C, P), low, after)

            def layer0_windows(n, i, j, end):
                u = 2 * i + j
                split, lo_split = split_counts(n, 0, u, end)
                dil_done = held(sp, 1 + tile(n, u, 0))
                l1_done = held(sp, 7 + n * NT)
                sp.wait_ge(dil_psum, dil_done)
                sp.wait_ge(l1_psum, l1_done)
                sp.wait_ge(hi_ready, split)
                sp.wait_ge(lo_ready, lo_split)
                copies(wins[j], (UPPER, LOWER), wins_in[j], u)
                copies(wins[j], (EVEN, ODD), dil_wins_in[j], u)

            def layer1_windows(n, r, slot, end):
                u = SLOTS * r + slot
                split, lo_split = split_counts(n, 1, u, end)
                dil_done = held(sp, 3 + (n + 1) * NT)
                l1_done = held(sp, 1 + tile(n, u, 0))
                sp.wait_ge(dil_psum, dil_done)
                sp.wait_ge(l1_psum, l1_done)
                sp.wait_ge(hi_ready, split)
                sp.wait_ge(lo_ready, lo_split)
                copies(l1_slot(slot), (UPPER, LOWER), l1_wins_in[slot], u)

            def store(n, u, j):
                made = [held(sp, 2 + tile(n, u, t) + 1) for t in range(TU)]
                for t in range(TU):
                    q = q_tile(u, t)
                    sp.wait_ge(out_ready, made[t])
                    sp.dma_start(out[n, :, q, :] if isinstance(n, int) else
                                 out[bass.ds(n, 1), :, q, :].rearrange("a p q w -> (a p) q w"),
                                 router_w[TU * j + t][:]).then_inc(out_st[TU * j + t], 16)

            def next_x(n, i, j):
                u = 2 * i + j
                outputs_made = held(sp, 2 + tile(n, u + 1, 0))
                loaded = held(sp, (n * NI + i + NI) * 16)
                sp.wait_ge(out_ready, outputs_made)
                sp.wait_ge(x_in[j], loaded)
                load_x(n + 1, u, j)

            def image_body(n, last):
                def step0(i, end=False):
                    layer0_windows(n, i, 0, False)
                    layer0_windows(n, i, 1, end)

                steps(sp, step0, 0, NI - 1)
                step0(NI - 1, True)

                def leave(r, slot):
                    if not last:
                        next_x(n, SLOTS // 2 * r + slot // 2, slot % 2)
                    store(n, SLOTS * r + slot, slot % 2)

                def round1(r, first=False, end=False):
                    for slot in range(SLOTS):
                        layer1_windows(n, r, slot, end and slot == SLOTS - 1)
                        if slot >= LAG:
                            leave(r, slot - LAG)
                        elif not first:
                            leave(r - 1, slot - LAG + SLOTS)

                round1(0, first=True)
                steps(sp, round1, 1, NR - 1)
                round1(NR - 1, end=True)
                for slot in range(SLOTS - LAG, SLOTS):
                    leave(NR - 1, slot)

            images(sp, image_body)
            for s_ in out_st:
                sp.wait_ge(s_, 16 + NS * NI * 16)

        @block.vector
        def _(dve):
            for s_, k in ((conv_free, 2), (comb_done, 2), (lo_ready, 2)):
                dve.sem_inc(s_, k)
            def tile_stats(u, t):
                nc.vector.bn_stats(bst[:, bass.ds(u * TU + t, 1), :].rearrange("p a s -> p (a s)"),
                                   image[:, q_tile(u, t), :].rearrange("p q w -> p (q w)")).then_inc(bst_step, 1)

            def x_stats(n, i):
                for j in range(2):
                    dve.wait_ge(x_in[j], (n * NI + i + 1) * 16)
                    for t in range(TU):
                        tile_stats(2 * i + j, t)

            nc.vector.memset(flat[:, 0:starts[-1]], 0.0).then_inc(stage_zero, 1)
            init = Order(dve, init_step, 0, 21)
            init.mark(nc.vector.memset(norm[:, 0, :, :], 0.0))
            init.mark(nc.vector.memset(norm[:, NQ + 1, :, :], 0.0))
            init.mark(nc.vector.memset(norm[:, 1:NQ + 1, :, 0:PADW], 0.0))
            init.mark(nc.vector.memset(norm[:, 1:NQ + 1, :, PADW + W:WP], 0.0))
            init.mark(nc.vector.memset(vsum[:, :, 0:1], 0.0))
            init.mark(nc.vector.memset(vsum[:, :, W + 1:W + 2], 0.0))
            init.mark(nc.vector.memset(beats1[:], 0.0))
            init.mark(nc.vector.memset(beats2[:], 0.0))
            for m, v in enumerate((2.0, 0.0, 0.0, 0.0, -1.0, 0.0, 1.0)):
                init.mark(nc.vector.memset(beats3[:, m, :], v))
            steps(dve, lambda i: x_stats(0, i), 0, NI)
            dve.wait_ge(taps_in, 16 * N_TAPS)
            dve.wait_ge(consts_in, 16 * len(small))
            for src, _ in STAGED:
                init.mark(nc.vector.tensor_scalar(src, src, W_SCALE, None, ALU.mult))
            init.wait()
            for src, dst in STAGED:
                nc.vector.tensor_copy(dst[HI], src).then_inc(split_w, 1)
            dve.wait_ge(split_w, len(STAGED))
            for src, dst in STAGED:
                nc.vector.tensor_tensor(dst[LO], src, dst[HI], ALU.subtract).then_inc(split_w, 1)
            init.mark(nc.vector.tensor_scalar(kbs[:], biases[:, 0:2], X_SCALE * W_SCALE, None, ALU.mult))
            init.mark(nc.vector.tensor_tensor(sb_sb[:], sb_sb[:], gb2_sb[:], ALU.add))
            dve.wait_ge(split_w, 2 * len(STAGED))
            init.wait()
            nc.vector.memset(rden[:], 0.0).then_inc(set_up, 1)
            init.close()

            def finish_stats(n, layer):
                s = Order(dve, stats_step, n * 2 + layer, 8)
                dve.wait_ge(bst_step, n * 2 * NT + layer * NT + NT)
                c = coef[layer]
                nc.vector.memset(T1, 0.0)
                nc.vector.bn_aggr(mv[:], bst[:].rearrange("p a s -> p (a s)")).then_inc(mean_in, 1)
                dve.wait_ge(mean_in, n * 2 + layer + 1)
                dve.wait_ge(stat_sum, n * 6 + layer * 4 + 1)
                s.mark(nc.vector.tensor_copy(MG, p_stat[:, 0:1]))
                s.wait()
                s.mark(nc.vector.tensor_tensor(D_, mv[:, 0:1], MG, ALU.subtract))
                s.wait()
                nc.vector.scalar_tensor_tensor(V2, D_, D_, mv[:, 1:2], ALU.mult, ALU.add).then_inc(sq_in, 1)
                dve.wait_ge(stat_sum, n * 6 + layer * 4 + 2)
                nc.vector.tensor_scalar(VE, p_stat[:, 1:2], GN_EPS, None, ALU.add).then_inc(sq_in, 1)
                dve.wait_ge(sq_done, n * 2 + layer + 1)
                s.mark(nc.vector.reciprocal(R_, SD))
                s.wait()
                s.mark(nc.vector.scalar_tensor_tensor(T1, R_, R_, VE, ALU.mult, ALU.mult))
                s.wait()
                s.mark(nc.vector.tensor_scalar(T2, T1, -0.5, 1.5, ALU.mult, ALU.add))
                s.wait()
                s.mark(nc.vector.tensor_tensor(c[:, 0:1], R_, T2, ALU.mult))
                s.wait()
                s.mark(nc.vector.scalar_tensor_tensor(c[:, 1:2], MG, -1.0, c[:, 0:1], ALU.mult, ALU.mult))
                s.mark(nc.vector.tensor_tensor(GN_, D_, c[:, 0:1], ALU.mult))
                s.wait()
                nc.vector.tensor_scalar(c[:, 2:4], c[:, 0:2], X_SCALE, None, ALU.mult).then_inc(coef_ready, 1)
                s.close()

            def gate(n):
                dve.wait_ge(hid_done, n + 1)
                nc.vector.tensor_copy(hid_rep[:], hid[:].to_broadcast([HID, P])).then_inc(sq_in, 1)
                dve.wait_ge(stat_sum, n * 6 + 4)
                nc.vector.tensor_tensor(rbias[:], p_stat[:, 4:8], sb_sb[:], ALU.add).then_inc(gate_ready, 1)

            def split_stages(n, layer, u):
                c = coef[layer]
                for t in range(TU):
                    k = n * 2 * NT + layer * NT + u * TU + t
                    dst = norm[:, bass.ds(u * QU + t * QT + 1, QT), :, PADW:PADW + W]
                    if dve_scales(layer, u):
                        dve.wait_ge(lo_ready, k + 1)
                        nc.vector.tensor_scalar(scaled[t][:], image[:, q_tile(u, t), :], c[:, 2:3], c[:, 3:4],
                                                ALU.mult, ALU.add).then_inc(scaled_ready, 1)
                    dve.wait_ge(scaled_ready, k + 1)
                    dve.wait_ge(hi_ready, k + 1)
                    nc.vector.tensor_tensor(dst[:, :, LO, :], scaled[t][:], dst[:, :, HI, :],
                                            ALU.subtract).then_inc(lo_ready, 1)
                    yield True

            def split_unit(n, layer, u):
                weave("ss", s=split_stages(n, layer, u))

            def router_stages(n, u):
                k = unit(n, u)
                s = Order(dve, router_step, k, 17)
                dve.wait_ge(logits_ready, k + 1)
                bias = rbias[:].rearrange("p (n o) -> p n o", o=1).to_broadcast([P, N_OPS, XCOLS])
                s.mark(nc.vector.scalar_tensor_tensor(logit[:], p_logit.rearrange("p x n -> p n x"),
                                                      1.0 / (X_SCALE * W_SCALE), bias, ALU.mult, ALU.add))
                yield True
                s.wait()
                for d, g in ((1, beats1), (2, beats2), (3, beats3)):
                    s.mark(nc.vector.tensor_tensor(g[:, d:N_OPS, :], logit[:, 0:N_OPS - d, :],
                                                   logit[:, d:N_OPS, :], ALU.is_ge))
                s.mark(nc.vector.tensor_tensor(top[:], logit[:, 0:2, :], logit[:, 2:4, :], ALU.max))
                yield True
                s.wait()
                s.mark(nc.vector.tensor_tensor(diff1[:], beats1[:, 1:N_OPS + 1, :], beats1[:, 0:N_OPS, :],
                                               ALU.subtract))
                s.mark(nc.vector.tensor_tensor(diff2[:], beats2[:, 2:N_OPS + 2, :], beats2[:, 0:N_OPS, :],
                                               ALU.subtract))
                s.mark(nc.vector.tensor_tensor(top[:, 0, :], top[:, 0, :], top[:, 1, :], ALU.max))
                yield True
                s.wait()
                s.mark(nc.vector.tensor_tensor(diff1[:], diff1[:], diff2[:], ALU.add))
                peak = top[:, 0:1, :].to_broadcast([P, N_OPS, XCOLS])
                nc.vector.tensor_tensor(logit[:], logit[:], peak, ALU.subtract).then_inc(exp_in, 1)
                yield True
                s.wait()
                s.mark(nc.vector.tensor_tensor(diff2[:], beats3[:, 3:N_OPS + 3, :], beats3[:, 0:N_OPS, :],
                                               ALU.subtract))
                yield True
                s.wait()
                s.mark(nc.vector.tensor_tensor(diff1[:], diff1[:], diff2[:], ALU.add))
                yield True
                s.wait()
                dve.wait_ge(exp_done, k + 1)
                s.mark(nc.vector.scalar_tensor_tensor(expo[:], diff1[:], 0.0, expo[:], ALU.is_ge, ALU.mult))
                yield True
                s.wait()
                s.mark(nc.vector.tensor_tensor(top[:], expo[:, 0:2, :], expo[:, 2:4, :], ALU.add))
                yield True
                s.wait()
                s.mark(nc.vector.tensor_tensor(top[:, 0, :], top[:, 0, :], top[:, 1, :], ALU.add))
                yield True
                s.wait()
                s.mark(nc.vector.reciprocal(rden[:], top[:, 0, :]))
                yield True
                s.wait()
                recip = rden[:].rearrange("p (o x) -> p o x", o=1).to_broadcast([P, N_OPS, XCOLS])
                s.mark(nc.vector.scalar_tensor_tensor(logit[:], expo[:], PROB_SCALE, recip, ALU.mult, ALU.mult))
                yield True
                s.wait()
                lg = logit[:].rearrange("p n (q b) -> p n q b", q=QU)
                px = w_px[:].rearrange("p n q a b -> p a n q b")
                s.mark(nc.vector.tensor_copy(px[:, HI], lg))
                yield True
                s.wait()
                nc.vector.tensor_tensor(px[:, LO], lg, px[:, HI], ALU.subtract).then_inc(probs_ready, 1)
                s.close()
                yield True

            def combine_stages(n, u, t):
                k = tile(n, u, t)
                s = Order(dve, comb_step, k, 3)
                dst = image[:, q_tile(u, t), :]
                dve.wait_ge(v1_psum, k + 1)
                dve.wait_ge(router_w_ready, 2 + 4 * k + 2)
                dve.wait_ge(comb_done, 2 + k)
                s.mark(nc.vector.scalar_tensor_tensor(prod[:], p_v1[t][:], kbs[:, 0:1], router_w[1][:],
                                                      ALU.add, ALU.mult))
                yield True
                dve.wait_ge(dil_psum, 3 + k + 1)
                dve.wait_ge(router_w_ready, 2 + 4 * k + 3)
                nc.vector.scalar_tensor_tensor(router_w[2][:], p_dil[t][:], kbs[:, 1:2], router_w[2][:],
                                               ALU.add, ALU.mult).then_inc(conv_free, 1)
                yield True
                dve.wait_ge(conv_free, 2 + k + 1)
                s.wait()
                s.mark(nc.vector.tensor_tensor(prod[:], prod[:], router_w[2][:], ALU.add))
                yield True
                dve.wait_ge(pool_ready, 1 + k + 1)
                s.wait()
                s.mark(nc.vector.tensor_tensor(prod[:], prod[:], pool_p[t][:], ALU.add))
                yield True
                dve.wait_ge(base_ready, k + 1)
                s.wait()
                nc.vector.tensor_tensor(dst, prod[:], base[t][:], ALU.add).then_inc(comb_done, 1)
                yield True
                dve.wait_ge(comb_done, 2 + k + 1)
                tile_stats(u, t)
                s.close()
                yield True

            def image_body(n, last):
                finish_stats(n, 0)
                dve.wait_ge(coef_ready, 2 * n + 1)
                for s_ in l1_wins_in:
                    dve.wait_ge(s_, l1_wins_count(n, 0))
                split_unit(n, 0, 0)
                split_unit(n, 0, 1)
                gate(n)
                dve.wait_ge(gate_ready, n + 1)
                weave("rrrrrrrrrrrrr", r=router_stages(n, 0))
                split_unit(n, 0, 2)
                split_unit(n, 0, 3)

                def step0(i, all_split, end):
                    for j in range(2):
                        u = 2 * i + j
                        if end and j == 1:
                            weave("cccccc", c=combine_stages(n, u, 0))
                        else:
                            weave("rrrcrcrrcrcrrcrcrrr", r=router_stages(n, u + 1), c=combine_stages(n, u, 0))
                        if all_split:
                            weave("cccccc", c=combine_stages(n, u, 1))
                        else:
                            weave("ccscccsc", c=combine_stages(n, u, 1), s=split_stages(n, 0, u + LEAD))

                all_steps(dve, step0)

                finish_stats(n, 1)
                dve.wait_ge(coef_ready, 2 * n + 2)
                for s_ in wins_in:
                    dve.wait_ge(s_, wins_count(n + 1, 0))
                for s_ in dil_wins_in:
                    dve.wait_ge(s_, dil_wins_count(n + 1, 0))
                split_unit(n, 1, 0)
                split_unit(n, 1, 1)
                steps(dve, lambda i: [split_unit(n, 1, 2 * i), split_unit(n, 1, 2 * i + 1)], 1, NI)
                if not last:
                    steps(dve, lambda i: x_stats(n + 1, i), 0, NI)

            images(dve, image_body)

        @block.scalar
        def _(act):
            for s_, k in ((router_w_ready, 2), (l1_evac, 2), (vsum_ready, 1)):
                act.sem_inc(s_, k)
            for s_ in out_st:
                act.sem_inc(s_, 16)
            act.wait_ge(set_up, 1)

            def stats_root(n, layer):
                act.wait_ge(sq_in, n * 5 + layer * 3 + 2)
                nc.scalar.activation(SD, VE, ACT.Sqrt).then_inc(sq_done, 1)

            def hi_unit(n, layer, u, tiles=range(TU)):
                c = coef[layer]
                for t in tiles:
                    k = n * 2 * NT + layer * NT + u * TU + t
                    if not dve_scales(layer, u):
                        act.wait_ge(lo_ready, k + 1)
                        nc.scalar.activation(scaled[t][:], image[:, q_tile(u, t), :], ACT.Identity,
                                             bias=c[:, 3:4], scale=c[:, 2:3]).then_inc(scaled_ready, 1)
                    nc.scalar.activation(norm[:, bass.ds(u * QU + t * QT + 1, QT), HI, PADW:PADW + W],
                                         image[:, q_tile(u, t), :], ACT.Identity, bias=c[:, 3:4],
                                         scale=c[:, 2:3]).then_inc(hi_ready, 1)

            def exps(n, u):
                act.wait_ge(exp_in, unit(n, u) + 1)
                nc.scalar.activation(expo[:], logit[:], ACT.Exp).then_inc(exp_done, 1)

            def weights_row(n, u):
                act.wait_ge(tr_ready, unit(n, u) + 1)
                nc.scalar.copy(w_row[:], p_tr).then_inc(w_row_ready, 1)

            UNSCALE = [1.0 / PROB_SCALE, 1.0 / (PROB_SCALE * X_SCALE * W_SCALE),
                       1.0 / (PROB_SCALE * X_SCALE * W_SCALE), 1.0 / (PROB_SCALE * X_SCALE * 9.0)]

            def normalised(n, u, t):
                k = tile(n, u, t)
                act.wait_ge(w0_used, 1 + k)
                nc.scalar.activation(xn[t][:], image[:, q_tile(u, t), :], ACT.Identity, bias=coef[0][:, 1:2],
                                     scale=coef[0][:, 0:1]).then_inc(xn_ready, 1)

            def vertical_sums(n, u, t):
                k = tile(n, u, t)
                act.wait_ge(pool_psum, k + 1)
                act.wait_ge(hsum_step, 2 * k + 2)
                nc.scalar.copy(vsum[:, :, 1:1 + W], p_pool[:]).then_inc(vsum_ready, 1)

            def op_weights(n, u, t, pair):
                k = tile(n, u, t)
                for m in (2 * pair, 2 * pair + 1):
                    act.wait_ge(pw_ready, 4 * k + m + 1)
                    if m == 0:
                        act.wait_ge(w0_used, 2 + k)
                    elif m == 3:
                        act.wait_ge(pool_ready, k + 1)
                    elif m == 1:
                        act.wait_ge(conv_free, k + 2)
                    elif m == 2:
                        act.wait_ge(comb_done, k + 2)
                    nc.scalar.activation(router_w[m][:], p_w[m % 2][:], ACT.Copy,
                                         scale=UNSCALE[m]).then_inc(router_w_ready, 1)

            def conv_out(n, u, t):
                k = tile(n, u, t)
                act.wait_ge(l1_psum, 7 + k + 1)
                act.wait_ge(out_ready, k + 1)
                nc.scalar.activation(xn[t][:], p_v1[t][:], ACT.Identity, bias=biases[:, 2:3],
                                     scale=1.0 / (X_SCALE * W_SCALE)).then_inc(l1_evac, 1)

            def image_body(n, last):
                stats_root(n, 0)
                act.wait_ge(coef_ready, 2 * n + 1)
                for s_ in l1_wins_in:
                    act.wait_ge(s_, l1_wins_count(n, 0))
                for s_ in out_st:
                    act.wait_ge(s_, stored_count(n, 0))
                hi_unit(n, 0, 0)
                act.wait_ge(stat_sum, n * 6 + 3)
                nc.scalar.activation(hid[:], p_stat[0:HID, 2:3], ACT.Relu, bias=gb1_sb[:],
                                     scale=1.0 / B4).then_inc(hid_done, 1)
                hi_unit(n, 0, 1)
                exps(n, 0)
                hi_unit(n, 0, 2)
                hi_unit(n, 0, 3)

                def step0(i, all_split, end):
                    for j in range(2):
                        u = 2 * i + j
                        normalised(n, u, 0)
                        vertical_sums(n, u, 0)
                        weights_row(n, u)
                        op_weights(n, u, 0, 0)
                        if not all_split:
                            hi_unit(n, 0, u + LEAD, (0,))
                        op_weights(n, u, 0, 1)
                        normalised(n, u, 1)
                        vertical_sums(n, u, 1)
                        if not (end and j == 1):
                            exps(n, u + 1)
                        op_weights(n, u, 1, 0)
                        if not all_split:
                            hi_unit(n, 0, u + LEAD, (1,))
                        op_weights(n, u, 1, 1)

                all_steps(act, step0)

                stats_root(n, 1)
                act.wait_ge(coef_ready, 2 * n + 2)
                for s_ in wins_in:
                    act.wait_ge(s_, wins_count(n + 1, 0))
                for s_ in dil_wins_in:
                    act.wait_ge(s_, dil_wins_count(n + 1, 0))
                for u in range(LEAD):
                    hi_unit(n, 1, u)

                def step1(i, all_split, end):
                    for j in range(2):
                        u = 2 * i + j
                        if not all_split:
                            hi_unit(n, 1, u + LEAD)
                        conv_out(n, u, 0)
                        conv_out(n, u, 1)

                all_steps(act, step1)

            images(act, image_body)

        @block.gpsimd
        def _(pool):
            for s_, k in ((hsum_step, 2), (w0_used, 2), (pool_ready, 1), (out_ready, 2)):
                pool.sem_inc(s_, k)
            pool.wait_ge(set_up, 1)

            def base_and_pool(n, u, t):
                k = tile(n, u, t)
                pool.wait_ge(xn_ready, k + 1)
                pool.wait_ge(comb_done, k + 1)
                pool.wait_ge(vsum_ready, 1 + k + 1)
                nc.gpsimd.tensor_tensor(pool_p[t][:], vsum[:, :, 0:W], vsum[:, :, 1:1 + W], ALU.add).then_inc(hsum_step, 1)
                pool.wait_ge(hsum_step, 2 + 2 * k + 1)
                nc.gpsimd.tensor_tensor(pool_p[t][:], pool_p[t][:], vsum[:, :, 2:2 + W], ALU.add).then_inc(hsum_step, 1)
                pool.wait_ge(router_w_ready, 2 + 4 * k + 1)
                nc.gpsimd.tensor_tensor(base[t][:], xn[t][:], router_w[0][:], ALU.mult).then_inc(w0_used, 1)
                pool.wait_ge(w0_used, 2 + k + 1)
                nc.gpsimd.tensor_tensor(base[t][:], base[t][:], image[:, q_tile(u, t), :],
                                        ALU.add).then_inc(base_ready, 1)
                pool.wait_ge(router_w_ready, 2 + 4 * k + 4)
                pool.wait_ge(hsum_step, 2 + 2 * k + 2)
                nc.gpsimd.tensor_tensor(pool_p[t][:], pool_p[t][:], router_w[3][:], ALU.mult).then_inc(pool_ready, 1)

            def residual(n, i, j, t):
                u = 2 * i + j
                k = tile(n, u, t)
                pool.wait_ge(l1_evac, 2 + k + 1)
                pool.wait_ge(out_st[TU * j + t], stored_count(n, i))
                nc.gpsimd.tensor_tensor(router_w[TU * j + t][:], xn[t][:], image[:, q_tile(u, t), :],
                                        ALU.add).then_inc(out_ready, 1)

            def image_body(n, last):
                def step0(i):
                    for j in range(2):
                        for t in range(TU):
                            base_and_pool(n, 2 * i + j, t)

                def step1(i):
                    for j in range(2):
                        for t in range(TU):
                            residual(n, i, j, t)

                steps(pool, step0, 0, NI)
                steps(pool, step1, 0, NI)

            images(pool, image_body)

        @block.tensor
        def _(pe):
            pe.sem_inc(dil_psum, 3)
            pe.sem_inc(l1_psum, 7)
            pe.wait_ge(set_up, 1)
            mm = nc.tensor.matmul

            def moving(win, kind, t, part_, kw, dil):
                off = PADW + (kw - 1) * dil
                return win[:, kind, t * QT:(t + 1) * QT, part_, off:off + W]

            def group_stats(n, layer):
                pe.wait_ge(mean_in, 2 * n + layer + 1)
                mm(p_stat[:, 0:1], avg_sb[:], mv[:, 0:1], start=True, stop=True).then_inc(stat_sum, 1)
                pe.wait_ge(sq_in, n * 5 + layer * 3 + 1)
                mm(p_stat[:, 1:2], avg_sb[:], V2, start=True, stop=True).then_inc(stat_sum, 1)

            def gate(n):
                pe.wait_ge(coef_ready, 2 * n + 1)
                mm(p_stat[0:HID, 2:3], gw1_sb[:], GN_, start=True, stop=True).then_inc(stat_sum, 1)
                pe.wait_ge(sq_in, n * 5 + 3)
                mm(p_stat[:, 4:8], hid_rep[:], gw2_sb[:], start=True, stop=True).then_inc(stat_sum, 1)

            def logits(n, u):
                both_parts = n * 2 * NT + (u + 1) * TU
                pe.wait_ge(hi_ready, both_parts)
                pe.wait_ge(lo_ready, both_parts + 2)
                for q in range(QU):
                    for h in range(HALVES):
                        for m, (xp, wp) in enumerate(PRODUCTS):
                            px = norm[:, bass.ds(u * QU + q + 1, 1), xp, PADW + h * P:PADW + h * P + P]
                            px = px.rearrange("p a w -> p (a w)")
                            last = mm(p_logit_qh[:, q, h], px, w_sw[:, wp, :],
                                      start=m == 0, stop=m == len(PRODUCTS) - 1)
                last.then_inc(logits_ready, 1)

            def transpose_weights(n, u):
                pe.wait_ge(probs_ready, unit(n, u) + 1)
                for h in range(HALVES):
                    src = w_px[:].rearrange("p n q a (b h) -> p h (n q a b)", h=HALVES)[:, h]
                    last = nc.tensor.transpose(p_tr[:, h * P:(h + 1) * P], src, idn[:])
                last.then_inc(tr_ready, 1)

            def vertical(dst, weights, win, t, parts):
                todo = [(kw, xp, wp) for kw in range(3) for xp, wp in parts]
                for m, (kw, xp, wp) in enumerate(todo):
                    for half, kind in enumerate((UPPER, LOWER)):
                        last = mm(dst[half * 2 * C:(half + 1) * 2 * C, :, :], weights[:, kw, wp, :],
                                  moving(win, kind, t, xp, kw, 1), start=m == 0, stop=m == len(todo) - 1)
                return last

            def vertical2(dst, win, t):
                todo = [(kw, xp, wp) for kw in range(3) for xp, wp in PRODUCTS]
                for m, (kw, xp, wp) in enumerate(todo):
                    for b in range(B4):
                        last = mm(dst[b * C:b * C + C, :, :], w_v2[:, kw, wp, C * (b // 2):C * (b // 2) + C],
                                  moving(win, (EVEN, ODD)[b % 2], t, xp, kw, 2), start=m == 0, stop=m == len(todo) - 1)
                    yield last

            def op_weights(n, u, t, pair):
                k = tile(n, u, t)
                pe.wait_ge(router_w_ready, 4 * k + 2 * pair + 2)
                for g in range(QT):
                    for m in (2 * pair, 2 * pair + 1):
                        rows = slice(m * K_OP, (m + 1) * K_OP)
                        spread = mm(p_w[m % 2][:, g, :], sel[rows, t * QT + g, :], w_row[rows, :],
                                    start=True, stop=True)
                        if g == QT - 1:
                            spread.then_inc(pw_ready, 1)

            def layer0_tile(n, u, j, t, route_next, dil_windows):
                k = tile(n, u, t)
                pe.wait_ge(vsum_ready, 1 + k)
                for m, xp in enumerate((HI, LO)):
                    for half, kind in enumerate((UPPER, LOWER)):
                        last = mm(p_pool[half * 2 * C:(half + 1) * 2 * C, :, :], w_pool[:],
                                  moving(wins[j], kind, t, xp, 1, 1), start=m == 0, stop=m == 1)
                last.then_inc(pool_psum, 1)
                pe.wait_ge(conv_free, k + 1)
                vertical(p_v1[t], w_v1, wins[j], t, PRODUCTS).then_inc(v1_psum, 1)
                if t == 0:
                    transpose_weights(n, u)
                pe.wait_ge(dil_wins_in[j], dil_windows)
                for m, last in enumerate(vertical2(p_dil[t], wins[j], t)):
                    if m == FIRST_W[t]:
                        if t == 0:
                            pe.wait_ge(w_row_ready, unit(n, u) + 1)
                        op_weights(n, u, t, 0)
                    elif m == SECOND_W[t]:
                        op_weights(n, u, t, 1)
                    elif m == LOGITS and route_next:
                        logits(n, u + 1)
                last.then_inc(dil_psum, 1)

            def image_body(n, last_image):
                group_stats(n, 0)
                gate(n)
                pe.wait_ge(gate_ready, n + 1)
                logits(n, 0)

                def step0(i, end=False):
                    for j in range(2):
                        u = 2 * i + j
                        more = not (end and j == 1)
                        pe.wait_ge(wins_in[j], wins_count(n, i + 1))
                        layer0_tile(n, u, j, 0, more, dil_wins_count(n, i + 1))
                        layer0_tile(n, u, j, 1, False, dil_wins_count(n, i + 1))

                steps(pe, step0, 0, NI - 1)
                step0(NI - 1, True)

                group_stats(n, 1)

                def round1(r):
                    for slot in range(SLOTS):
                        u = SLOTS * r + slot
                        pe.wait_ge(l1_wins_in[slot], l1_wins_count(n, r + 1))
                        for t in range(TU):
                            k = tile(n, u, t)
                            pe.wait_ge(l1_evac, k + 1)
                            vertical(p_v1[t], w_l1, l1_slot(slot), t, PRODUCTS).then_inc(l1_psum, 1)

                steps(pe, round1, 0, NR)

            images(pe, image_body)


def layout(inputs):
    x = np.asarray(inputs["x"])
    n, c, h, w = x.shape
    q = h // B4
    g = {k: np.asarray(v) for k, v in inputs.items()}
    taps = lambda a: np.ascontiguousarray(a.transpose(1, 2, 3, 0))
    per_partition = lambda a: np.ascontiguousarray(np.tile(a, B4)[:, None])
    everywhere = lambda a: np.ascontiguousarray(np.tile(a[None, :], (P, 1)))
    avg = np.zeros((P, P), np.float32)
    group = (np.arange(P) % C) // 2
    avg[group[:, None] == group[None, :]] = 1.0 / (2 * B4)
    ident = np.eye(P, dtype=np.float16)
    select = np.zeros((N_OPS, QU, 2, B4, QU, P), np.float16)
    for qq in range(QU):
        for b in range(B4):
            select[:, qq, :, b, qq, C * b:C * b + C] = 1
    vpool = np.zeros((P, 2 * C), np.float16)
    for k, b, _ in vertical_taps():
        vpool[C * k + np.arange(C), C * b + np.arange(C)] = 1
    return {
        "x": np.ascontiguousarray(x.reshape(n, c, q, B4, w).transpose(0, 3, 1, 2, 4)).reshape(n, P, q, w),
        "gw1t": np.ascontiguousarray(g["L0_conv_gw1"].T), "gb1": np.ascontiguousarray(g["L0_conv_gb1"][:, None]),
        "gw2t": np.ascontiguousarray(g["L0_conv_gw2"].T), "gb2": everywhere(g["L0_conv_gb2"]),
        "sb_": everywhere(g["L0_conv_sb"]), "swt": np.ascontiguousarray(g["L0_conv_sw"].T),
        "k1t": taps(g["L0_conv_k1"]), "kb1": per_partition(g["L0_conv_kb1"]),
        "k2t": taps(g["L0_conv_k2"]), "kb2": per_partition(g["L0_conv_kb2"]),
        "l1t": taps(g["L1_conv_weight"]), "l1b": per_partition(g["L1_conv_bias"]),
        "avg": avg, "ident": ident, "select": select.reshape(P, -1), "vpool": vpool,
    }


def kernel(**inputs):
    import concourse.bacc as _bacc
    from concourse.bass_utils import run_bass_kernel_spmd as _run

    nc = _bacc.Bacc("TRN2", target_bir_lowering=False, num_devices=1)
    arrays = layout(inputs)
    args = {k: nc.dram_tensor(f"in_{k}", a.shape, mybir.dt.from_np(a.dtype), kind="ExternalInput").ap()
            for k, a in arrays.items()}
    n, p, q, w = arrays["x"].shape
    out = nc.dram_tensor("out_y", (n, p, q, w), F32, kind="ExternalOutput").ap()
    build(nc, out=out, **args)
    r = _run(nc, [{f"in_{k}": a for k, a in arrays.items()}], core_ids=[0])
    y = r.results[0]["out_y"]
    return y.reshape(n, B4, C, q, w).transpose(0, 2, 3, 1, 4).reshape(n, C, q * B4, w)
```
